# Optimizing a Trainium2 kernel written in Bass

```python
import numpy as np
import jax
import jax.numpy as jnp

def _softmax(x, axis=-1):
    return jax.nn.softmax(x, axis=axis)

def _gelu(x):
    return jax.nn.gelu(x, approximate=True)

def _silu(x):
    return jax.nn.silu(x)

def _sigmoid(x):
    return jax.nn.sigmoid(x)

def _layernorm(x, axis=-1, eps=1e-05):
    m = jnp.mean(x, axis=axis, keepdims=True)
    v = jnp.var(x, axis=axis, keepdims=True)
    return (x - m) / jnp.sqrt(v + eps)

def _scatter_add(tgt, idx, src, axis=0):
    return tgt.at[idx].add(src)

def _segment_sum(src, seg, n):
    return jax.ops.segment_sum(src, seg, n)
kernel_name = 'mk_gnn_resnorm_d4_gnn_r32_58aa83'

def setup_inputs(seed: int=0):
    np.random.seed(seed)
    _w = jnp.asarray

    def _rec_inputs():
        import jax
        import jax.numpy as jnp
        _gk = jax.random.key(seed)
        x = -0.0003713 + 1 * jax.random.normal(jax.random.fold_in(_gk, 1), (3125, 128), jnp.float32)
        src = jax.random.randint(jax.random.fold_in(_gk, 2), (100000,), 0, 3125, jnp.int32)
        dst = jax.random.randint(jax.random.fold_in(_gk, 3), (100000,), 0, 3125, jnp.int32)
        _o = jnp.argsort(dst, stable=True)
        src = src[_o]
        dst = dst[_o]
        edge_attr_9 = 0.000458729 + 1.00015 * jax.random.normal(jax.random.fold_in(_gk, 11), (100000, 9), jnp.float32)
        edge_weight = jax.random.uniform(jax.random.fold_in(_gk, 13), (100000,), jnp.float32, 0.0, 0.999998)
        return (x, src, dst, edge_attr_9, edge_weight)
    x, src, dst, edge_attr_9, edge_weight = _rec_inputs()

    def _L0_gnn_setup():
        import jax, jax.numpy as jnp
        import numpy as np
        N = 3125
        E = 50000
        D = 128
        H = 128

        def gcn_conv(x, W, b, src, dst, n_nodes):
            h = x @ W
            loop = jnp.arange(n_nodes, dtype=src.dtype)
            s = jnp.concatenate([src, loop])
            d = jnp.concatenate([dst, loop])
            deg = jnp.zeros((n_nodes,), dtype=h.dtype).at[d].add(1.0)
            dinv = jnp.where(deg > 0, jax.lax.rsqrt(deg), 0.0)
            norm = dinv[s] * dinv[d]
            msg = h[s] * norm[:, None]
            out = jax.ops.segment_sum(msg, d, num_segments=n_nodes)
            return out + b
        key = jax.random.key(seed)
        ks = jax.random.split(key, 8)
        x = jax.random.normal(ks[0], (N, D), dtype=jnp.float32)
        edge_index = jax.random.randint(ks[1], (2, E), 0, N, dtype=jnp.int32)
        sc = 1.0 / np.sqrt(D)
        gate_W = jax.random.uniform(ks[2], (D, D), jnp.float32, -sc, sc)
        gate_b = jax.random.uniform(ks[3], (D,), jnp.float32, -sc, sc)
        W1 = jax.random.normal(ks[4], (D, H), dtype=jnp.float32) * sc
        b1 = jnp.zeros((H,), jnp.float32)
        W2 = jax.random.normal(ks[5], (H, H), dtype=jnp.float32) * (1.0 / np.sqrt(H))
        b2 = jnp.zeros((H,), jnp.float32)
        return {'x': x, 'edge_index': edge_index, 'gate_W': gate_W, 'gate_b': gate_b, 'W1': W1, 'b1': b1, 'W2': W2, 'b2': b2}
    _L0_gnn_all = _L0_gnn_setup()
    _L0_gnn_in = {k: v for k, v in _L0_gnn_all.items() if k in ('gate_W', 'gate_b', 'W1', 'b1', 'W2', 'b2')}
    del _L0_gnn_all

    def _L1_gnn_setup():
        import jax, jax.numpy as jnp
        import numpy as np
        N_NODES = 3125
        N_EDGES = 20000
        DIM = 128
        key = jax.random.key(seed)
        k1, k2, k3, k4, k5 = jax.random.split(key, 5)
        x = jax.random.normal(k1, (N_NODES, DIM), dtype=jnp.float32)
        edge_index = jax.random.randint(k2, (2, N_EDGES), 0, N_NODES, dtype=jnp.int64)
        edge_weight = jax.random.uniform(k3, (N_EDGES,), dtype=jnp.float32)
        W = jax.random.normal(k4, (DIM, DIM), dtype=jnp.float32) * (1.0 / np.sqrt(DIM))
        b = jax.random.normal(k5, (DIM,), dtype=jnp.float32) * 0.01
        return {'x': x, 'edge_index': edge_index, 'edge_weight': edge_weight, 'W': W, 'b': b}
    _L1_gnn_all = _L1_gnn_setup()
    _L1_gnn_in = {k: v for k, v in _L1_gnn_all.items() if k in ('W', 'b')}
    del _L1_gnn_all

    def _L2_gnn_setup():
        import jax, jax.numpy as jnp
        import numpy as np
        N = 50000
        E = 25000
        D_IN = 128
        D_H = 256

        def gcn_conv(x, W, b, src, dst, deg_inv_sqrt, n):
            h = x @ W
            norm = deg_inv_sqrt[src] * deg_inv_sqrt[dst]
            msg = h[src] * norm[:, None]
            out = jax.ops.segment_sum(msg, dst, num_segments=n)
            return out + b
        key = jax.random.key(seed)
        ks = jax.random.split(key, 12)
        inp = {'x': jax.random.normal(ks[0], (N, D_IN), dtype=jnp.float32), 'edge_index': jax.random.randint(ks[1], (2, E), 0, N, dtype=jnp.int32)}
        dims = [(D_IN, D_H), (D_H, D_H), (D_H, D_H), (D_H, D_IN)]
        for i, (din, dout) in enumerate(dims):
            scale = 1.0 / np.sqrt(din)
            inp[f'W{i}'] = jax.random.uniform(ks[2 + 2 * i], (din, dout), dtype=jnp.float32, minval=-scale, maxval=scale)
            inp[f'b{i}'] = jnp.zeros((dout,), dtype=jnp.float32)
        return inp
    _L2_gnn_all = _L2_gnn_setup()
    _L2_gnn_in = {k: v for k, v in _L2_gnn_all.items() if k in ('W0', 'b0', 'W1', 'b1', 'W2', 'b2', 'W3', 'b3')}
    del _L2_gnn_all

    def _L3_gnn_setup():
        import jax, jax.numpy as jnp
        import numpy as np
        from fractions import Fraction
        from math import factorial

        def _su2_cg_coeff(j1, m1, j2, m2, j3, m3):
            if m3 != m1 + m2:
                return 0.0
            vmin = int(max(-j1 + j2 + m3, -j1 + m1, 0))
            vmax = int(min(j2 + j3 + m1, j3 - j1 + j2, j3 + m3))
            f = lambda n: factorial(round(n))
            C = ((2.0 * j3 + 1.0) * Fraction(f(j3 + j1 - j2) * f(j3 - j1 + j2) * f(j1 + j2 - j3) * f(j3 + m3) * f(j3 - m3), f(j1 + j2 + j3 + 1) * f(j1 - m1) * f(j1 + m1) * f(j2 - m2) * f(j2 + m2))) ** 0.5
            S = 0
            for v in range(vmin, vmax + 1):
                S += (-1) ** (v + j2 + m2) * Fraction(f(j2 + j3 + m1 - v) * f(j1 - m1 + v), f(v) * f(j3 - j1 + j2 - v) * f(j3 + m3 - v) * f(v + j1 - j2 - m3))
            return float(C * S)

        def _change_basis_real_to_complex(l):
            q = np.zeros((2 * l + 1, 2 * l + 1), dtype=np.complex128)
            for m in range(-l, 0):
                q[l + m, l + abs(m)] = 1 / np.sqrt(2)
                q[l + m, l - abs(m)] = -1j / np.sqrt(2)
            q[l, l] = 1
            for m in range(1, l + 1):
                q[l + m, l + abs(m)] = (-1) ** m / np.sqrt(2)
                q[l + m, l - abs(m)] = 1j * (-1) ** m / np.sqrt(2)
            return (-1j) ** l * q

        def wigner_3j(l1, l2, l3):
            C = np.zeros((2 * l1 + 1, 2 * l2 + 1, 2 * l3 + 1))
            for m1 in range(-l1, l1 + 1):
                for m2 in range(-l2, l2 + 1):
                    m3 = m1 + m2
                    if abs(m3) <= l3:
                        C[l1 + m1, l2 + m2, l3 + m3] = _su2_cg_coeff(l1, m1, l2, m2, l3, m3)
            Q1 = _change_basis_real_to_complex(l1)
            Q2 = _change_basis_real_to_complex(l2)
            Q3 = _change_basis_real_to_complex(l3)
            Cc = np.einsum('ij,kl,mn,ikn->jlm', Q1, Q2, np.conj(Q3.T), C.astype(np.complex128))
            Cr = np.real(Cc)
            return Cr / np.linalg.norm(Cr)
        MUL = 32
        IRREPS_IN = [(MUL, 0, 1), (MUL, 1, -1)]
        IRREPS_SH = [(1, 0, 1), (1, 1, -1), (1, 2, 1)]
        IRREPS_OUT = [(MUL, 0, 1), (MUL, 1, -1)]
        NUM_NEIGHBORS = 10.0
        N_NODES, N_EDGES = (10000, 3125)

        def _dim(irreps):
            return sum((m * (2 * l + 1) for m, l, _ in irreps))

        def _slices(irreps):
            s, out = (0, [])
            for m, l, _ in irreps:
                d = m * (2 * l + 1)
                out.append((s, s + d))
                s += d
            return out

        def _instructions():
            ins = []
            for i1, (m1, l1, p1) in enumerate(IRREPS_IN):
                for i2, (m2, l2, p2) in enumerate(IRREPS_SH):
                    for io, (mo, lo, po) in enumerate(IRREPS_OUT):
                        if abs(l1 - l2) <= lo <= l1 + l2 and p1 * p2 == po:
                            ins.append((i1, i2, io))
            return ins
        _INSTR = _instructions()
        _SL_IN, _SL_SH, _SL_OUT = (_slices(IRREPS_IN), _slices(IRREPS_SH), _slices(IRREPS_OUT))
        _W3J = [jnp.asarray(wigner_3j(IRREPS_IN[i1][1], IRREPS_SH[i2][1], IRREPS_OUT[io][1]), dtype=jnp.float32) for i1, i2, io in _INSTR]
        _NORM = []
        for _i1, _i2, _io in _INSTR:
            _alpha = 2 * IRREPS_OUT[_io][1] + 1
            _x = sum((IRREPS_IN[j1][0] * IRREPS_SH[j2][0] for j1, j2, jo in _INSTR if jo == _io))
            _NORM.append(float(np.sqrt(_alpha / _x)))

        def _tensor_product(x1, x2, weights):
            E = x1.shape[0]
            out = jnp.zeros((E, _dim(IRREPS_OUT)), dtype=x1.dtype)
            for k, (i1, i2, io) in enumerate(_INSTR):
                m1, l1, _ = IRREPS_IN[i1]
                m2, l2, _ = IRREPS_SH[i2]
                mo, lo, _ = IRREPS_OUT[io]
                a, b = _SL_IN[i1]
                c, d = _SL_SH[i2]
                e, f = _SL_OUT[io]
                x1s = x1[:, a:b].reshape(E, m1, 2 * l1 + 1)
                x2s = x2[:, c:d].reshape(E, m2, 2 * l2 + 1)
                seg = jnp.einsum('uvw,ijk,eui,evj->ewk', weights[k], _W3J[k], x1s, x2s, optimize='optimal') * _NORM[k]
                out = out.at[:, e:f].add(seg.reshape(E, mo * (2 * lo + 1)))
            return out
        key = jax.random.key(seed)
        ks = jax.random.split(key, 8)
        x = jax.random.normal(ks[0], (N_NODES, _dim(IRREPS_IN)), dtype=jnp.float32)
        edge_index = jax.random.randint(ks[1], (2, N_EDGES), 0, N_NODES)
        edge_attr = jax.random.normal(ks[2], (N_EDGES, _dim(IRREPS_SH)), dtype=jnp.float32)
        ws = {f'w{k}': jax.random.normal(ks[3 + k], (MUL, 1, MUL), dtype=jnp.float32) for k in range(len(_INSTR))}
        return {'x': x, 'edge_index': edge_index, 'edge_attr': edge_attr, **ws}
    _L3_gnn_all = _L3_gnn_setup()
    _L3_gnn_in = {k: v for k, v in _L3_gnn_all.items() if k in ('w0', 'w1', 'w2', 'w3', 'w4')}
    del _L3_gnn_all
    return {'x': x, 'src': src, 'dst': dst, 'edge_attr_9': edge_attr_9, 'edge_weight': edge_weight, 'L0_gnn_gate_W': _L0_gnn_in['gate_W'], 'L0_gnn_gate_b': _L0_gnn_in['gate_b'], 'L0_gnn_W1': _L0_gnn_in['W1'], 'L0_gnn_b1': _L0_gnn_in['b1'], 'L0_gnn_W2': _L0_gnn_in['W2'], 'L0_gnn_b2': _L0_gnn_in['b2'], 'L1_gnn_W': _L1_gnn_in['W'], 'L1_gnn_b': _L1_gnn_in['b'], 'L2_gnn_W0': _L2_gnn_in['W0'], 'L2_gnn_b0': _L2_gnn_in['b0'], 'L2_gnn_W1': _L2_gnn_in['W1'], 'L2_gnn_b1': _L2_gnn_in['b1'], 'L2_gnn_W2': _L2_gnn_in['W2'], 'L2_gnn_b2': _L2_gnn_in['b2'], 'L2_gnn_W3': _L2_gnn_in['W3'], 'L2_gnn_b3': _L2_gnn_in['b3'], 'L3_gnn_w0': _L3_gnn_in['w0'], 'L3_gnn_w1': _L3_gnn_in['w1'], 'L3_gnn_w2': _L3_gnn_in['w2'], 'L3_gnn_w3': _L3_gnn_in['w3'], 'L3_gnn_w4': _L3_gnn_in['w4']}

def reference(x, src, dst, edge_attr_9, edge_weight, L0_gnn_gate_W, L0_gnn_gate_b, L0_gnn_W1, L0_gnn_b1, L0_gnn_W2, L0_gnn_b2, L1_gnn_W, L1_gnn_b, L2_gnn_W0, L2_gnn_b0, L2_gnn_W1, L2_gnn_b1, L2_gnn_W2, L2_gnn_b2, L2_gnn_W3, L2_gnn_b3, L3_gnn_w0, L3_gnn_w1, L3_gnn_w2, L3_gnn_w3, L3_gnn_w4):
    import jax
    import jax.numpy as jnp

    def _L0_gnn_ref(x, edge_index, gate_W, gate_b, W1, b1, W2, b2):
        import jax, jax.numpy as jnp
        import numpy as np
        N = 3125
        E = 50000
        D = 128
        H = 128

        def gcn_conv(x, W, b, src, dst, n_nodes):
            h = x @ W
            loop = jnp.arange(n_nodes, dtype=src.dtype)
            s = jnp.concatenate([src, loop])
            d = jnp.concatenate([dst, loop])
            deg = jnp.zeros((n_nodes,), dtype=h.dtype).at[d].add(1.0)
            dinv = jnp.where(deg > 0, jax.lax.rsqrt(deg), 0.0)
            norm = dinv[s] * dinv[d]
            msg = h[s] * norm[:, None]
            out = jax.ops.segment_sum(msg, d, num_segments=n_nodes)
            return out + b
        src, dst = (edge_index[0], edge_index[1])
        gate = jax.nn.sigmoid(x @ gate_W + gate_b)
        h = x * gate
        h = gcn_conv(h, W1, b1, src, dst, N)
        h = jax.nn.relu(h)
        h = gcn_conv(h, W2, b2, src, dst, N)
        return h

    def _L1_gnn_ref(x, edge_index, edge_weight, W, b):
        import jax, jax.numpy as jnp
        import numpy as np
        N_NODES = 3125
        N_EDGES = 20000
        DIM = 128
        row, col = (edge_index[0], edge_index[1])
        msgs = edge_weight[:, None] * x[row]
        agg = jax.ops.segment_sum(msgs, col, num_segments=x.shape[0])
        return agg @ W.T + b

    def _L2_gnn_ref(x, edge_index, W0, b0, W1, b1, W2, b2, W3, b3):
        import jax, jax.numpy as jnp
        import numpy as np
        N = 50000
        E = 25000
        D_IN = 128
        D_H = 256

        def gcn_conv(x, W, b, src, dst, deg_inv_sqrt, n):
            h = x @ W
            norm = deg_inv_sqrt[src] * deg_inv_sqrt[dst]
            msg = h[src] * norm[:, None]
            out = jax.ops.segment_sum(msg, dst, num_segments=n)
            return out + b
        n = x.shape[0]
        loops = jnp.arange(n, dtype=edge_index.dtype)
        src = jnp.concatenate([edge_index[0], loops])
        dst = jnp.concatenate([edge_index[1], loops])
        deg = jax.ops.segment_sum(jnp.ones(src.shape, x.dtype), dst, num_segments=n)
        deg_inv_sqrt = jnp.where(deg > 0, jax.lax.rsqrt(deg), 0.0)
        h = x
        for W, b in ((W0, b0), (W1, b1), (W2, b2), (W3, b3)):
            h = jax.nn.relu(gcn_conv(h, W, b, src, dst, deg_inv_sqrt, n))
        return h

    def _L3_gnn_ref(x, edge_index, edge_attr, w0, w1, w2, w3, w4):
        import jax, jax.numpy as jnp
        import numpy as np
        from fractions import Fraction
        from math import factorial

        def _su2_cg_coeff(j1, m1, j2, m2, j3, m3):
            if m3 != m1 + m2:
                return 0.0
            vmin = int(max(-j1 + j2 + m3, -j1 + m1, 0))
            vmax = int(min(j2 + j3 + m1, j3 - j1 + j2, j3 + m3))
            f = lambda n: factorial(round(n))
            C = ((2.0 * j3 + 1.0) * Fraction(f(j3 + j1 - j2) * f(j3 - j1 + j2) * f(j1 + j2 - j3) * f(j3 + m3) * f(j3 - m3), f(j1 + j2 + j3 + 1) * f(j1 - m1) * f(j1 + m1) * f(j2 - m2) * f(j2 + m2))) ** 0.5
            S = 0
            for v in range(vmin, vmax + 1):
                S += (-1) ** (v + j2 + m2) * Fraction(f(j2 + j3 + m1 - v) * f(j1 - m1 + v), f(v) * f(j3 - j1 + j2 - v) * f(j3 + m3 - v) * f(v + j1 - j2 - m3))
            return float(C * S)

        def _change_basis_real_to_complex(l):
            q = np.zeros((2 * l + 1, 2 * l + 1), dtype=np.complex128)
            for m in range(-l, 0):
                q[l + m, l + abs(m)] = 1 / np.sqrt(2)
                q[l + m, l - abs(m)] = -1j / np.sqrt(2)
            q[l, l] = 1
            for m in range(1, l + 1):
                q[l + m, l + abs(m)] = (-1) ** m / np.sqrt(2)
                q[l + m, l - abs(m)] = 1j * (-1) ** m / np.sqrt(2)
            return (-1j) ** l * q

        def wigner_3j(l1, l2, l3):
            C = np.zeros((2 * l1 + 1, 2 * l2 + 1, 2 * l3 + 1))
            for m1 in range(-l1, l1 + 1):
                for m2 in range(-l2, l2 + 1):
                    m3 = m1 + m2
                    if abs(m3) <= l3:
                        C[l1 + m1, l2 + m2, l3 + m3] = _su2_cg_coeff(l1, m1, l2, m2, l3, m3)
            Q1 = _change_basis_real_to_complex(l1)
            Q2 = _change_basis_real_to_complex(l2)
            Q3 = _change_basis_real_to_complex(l3)
            Cc = np.einsum('ij,kl,mn,ikn->jlm', Q1, Q2, np.conj(Q3.T), C.astype(np.complex128))
            Cr = np.real(Cc)
            return Cr / np.linalg.norm(Cr)
        MUL = 32
        IRREPS_IN = [(MUL, 0, 1), (MUL, 1, -1)]
        IRREPS_SH = [(1, 0, 1), (1, 1, -1), (1, 2, 1)]
        IRREPS_OUT = [(MUL, 0, 1), (MUL, 1, -1)]
        NUM_NEIGHBORS = 10.0
        N_NODES, N_EDGES = (10000, 3125)

        def _dim(irreps):
            return sum((m * (2 * l + 1) for m, l, _ in irreps))

        def _slices(irreps):
            s, out = (0, [])
            for m, l, _ in irreps:
                d = m * (2 * l + 1)
                out.append((s, s + d))
                s += d
            return out

        def _instructions():
            ins = []
            for i1, (m1, l1, p1) in enumerate(IRREPS_IN):
                for i2, (m2, l2, p2) in enumerate(IRREPS_SH):
                    for io, (mo, lo, po) in enumerate(IRREPS_OUT):
                        if abs(l1 - l2) <= lo <= l1 + l2 and p1 * p2 == po:
                            ins.append((i1, i2, io))
            return ins
        _INSTR = _instructions()
        _SL_IN, _SL_SH, _SL_OUT = (_slices(IRREPS_IN), _slices(IRREPS_SH), _slices(IRREPS_OUT))
        _W3J = [jnp.asarray(wigner_3j(IRREPS_IN[i1][1], IRREPS_SH[i2][1], IRREPS_OUT[io][1]), dtype=jnp.float32) for i1, i2, io in _INSTR]
        _NORM = []
        for _i1, _i2, _io in _INSTR:
            _alpha = 2 * IRREPS_OUT[_io][1] + 1
            _x = sum((IRREPS_IN[j1][0] * IRREPS_SH[j2][0] for j1, j2, jo in _INSTR if jo == _io))
            _NORM.append(float(np.sqrt(_alpha / _x)))

        def _tensor_product(x1, x2, weights):
            E = x1.shape[0]
            out = jnp.zeros((E, _dim(IRREPS_OUT)), dtype=x1.dtype)
            for k, (i1, i2, io) in enumerate(_INSTR):
                m1, l1, _ = IRREPS_IN[i1]
                m2, l2, _ = IRREPS_SH[i2]
                mo, lo, _ = IRREPS_OUT[io]
                a, b = _SL_IN[i1]
                c, d = _SL_SH[i2]
                e, f = _SL_OUT[io]
                x1s = x1[:, a:b].reshape(E, m1, 2 * l1 + 1)
                x2s = x2[:, c:d].reshape(E, m2, 2 * l2 + 1)
                seg = jnp.einsum('uvw,ijk,eui,evj->ewk', weights[k], _W3J[k], x1s, x2s, optimize='optimal') * _NORM[k]
                out = out.at[:, e:f].add(seg.reshape(E, mo * (2 * lo + 1)))
            return out
        i, j = (edge_index[0], edge_index[1])
        summand = _tensor_product(x[i], edge_attr, [w0, w1, w2, w3, w4])
        out = jax.ops.segment_sum(summand, j, num_segments=x.shape[0])
        return out / float(np.sqrt(NUM_NEIGHBORS))
    edge_index = jnp.stack([src, dst])
    x = _layernorm(x + _L0_gnn_ref(x, edge_index, L0_gnn_gate_W, L0_gnn_gate_b, L0_gnn_W1, L0_gnn_b1, L0_gnn_W2, L0_gnn_b2), axis=-1)
    x = _layernorm(x + _L1_gnn_ref(x, edge_index, edge_weight, L1_gnn_W, L1_gnn_b), axis=-1)
    x = _layernorm(x + _L2_gnn_ref(x, edge_index, L2_gnn_W0, L2_gnn_b0, L2_gnn_W1, L2_gnn_b1, L2_gnn_W2, L2_gnn_b2, L2_gnn_W3, L2_gnn_b3), axis=-1)
    x = _layernorm(x + _L3_gnn_ref(x, edge_index, edge_attr_9, L3_gnn_w0, L3_gnn_w1, L3_gnn_w2, L3_gnn_w3, L3_gnn_w4), axis=-1)
    return x

_drawn_inputs = setup_inputs


def setup_inputs(seed=0):
    import zlib

    import numpy as np

    out = dict(_drawn_inputs(seed))
    spreads = {'L0_gnn_b1': (0.0, 0.1),
     'L0_gnn_b2': (0.0, 0.1),
     'L2_gnn_b0': (0.0, 0.8),
     'L2_gnn_b1': (0.0, 0.8),
     'L2_gnn_b2': (0.0, 0.894),
     'L2_gnn_b3': (0.0, 0.318)}
    factors = {'L0_gnn_gate_b': 57.814,
     'L1_gnn_b': 8.0,
     'L2_gnn_W0': 7.541,
     'L2_gnn_W1': 6.367,
     'L2_gnn_W2': 3.988}
    for name, (base, spread) in spreads.items():
        noise = np.random.default_rng([zlib.crc32(name.encode()), seed]).standard_normal(out[name].shape)
        drawn = base * np.exp(spread * noise) if base else spread * noise
        out[name] = jnp.asarray(drawn.astype(out[name].dtype))
    for name, factor in factors.items():
        out[name] = (out[name] * factor).astype(out[name].dtype)
    return out
```

```python
from contextlib import ExitStack

import concourse.bass as bass
from concourse import mybir

F32 = mybir.dt.float32
BF16 = mybir.dt.bfloat16
F16 = mybir.dt.float16
I32 = mybir.dt.int32
U32 = mybir.dt.uint32
ALU = mybir.AluOpType
ACT = mybir.ActivationFunctionType
AX = mybir.AxisListType
RMAX = bass.bass_isa.ReduceOp.max
RADD = bass.bass_isa.ReduceOp.add

P = 128
D = 128
N = 3125
E = 100000
NB = -(-N // P)
LAST = N - (NB - 1) * P
CW = 512
NCH = -(-N // CW)
GT = 4
NG = -(-E // (P * GT))
NT = NG * GT
WIN = 22
SW = N + WIN + 1
NLOOP = NB
FAR = 8192
HB = 13
CODES = NB * WIN
EXACT = 256
BG = 8
NDB = NG // 2 // BG
NDG = NDB * BG
NGG = NG - NDG
BW = 152
DT = NDG * GT
NLO = 3
SPILL = 12
ACW = N + BW + 3
NJ = 9
LN_EPS = 1e-5
NPARTS = 3
ROWW = NPARTS * D
NEIGHBORS = 10.0


class Counter:

    def __init__(self, sem):
        self.sem, self.value = sem, 0


class Engine:

    def __init__(self):
        self.steps = []

    def wait(self, *tokens):
        for token in tokens:
            if token is not None:
                self.steps.append(lambda e, t=token: e.wait_ge(t[0], t[1]))

    def run(self, fn, counter=None, by=1):
        if counter is None:
            self.steps.append(fn)
            return None
        counter.value += by
        self.steps.append(lambda e: fn(e).then_inc(counter.sem, by))
        return (counter.sem, counter.value)

    def chain(self, counter, *fns):
        token = None
        for fn in fns:
            self.wait(token)
            token = self.run(fn, counter)
        return token

    def emit(self, engine):
        self.flag = None
        for step in self.steps:
            step(engine)


class Between:

    def __init__(self, prepare, finish):
        self.prepare, self.finish = prepare, finish


def chunk_shape(c):
    if (c + 1) * CW <= N:
        return CW // P, P, CW
    assert N - c * CW == LAST
    return 1, LAST, LAST


def build_program(nc, a):
    with ExitStack() as ctx:
        def sb(name, shape, dt):
            return ctx.enter_context(nc.sbuf_tensor(name, shape, dt))

        def counter(name):
            return Counter(ctx.enter_context(nc.semaphore(name)))

        pe, dve, act, pool, sp = Engine(), Engine(), Engine(), Engine(), Engine()

        narrow_tab = [nc.dram_tensor(f"narrow_tab{i}", (N, ROWW), BF16, kind="Internal").ap() for i in range(2)]
        wide_tab = [nc.dram_tensor(f"wide_tab{i}", (N, 2 * ROWW), BF16, kind="Internal").ap() for i in range(2)]
        x_tab = [nc.dram_tensor(f"x_tab{i}", (N, D), F32, kind="Internal").ap() for i in range(3)]
        code_tab = nc.dram_tensor("code_tab", (P, DT), F32, kind="Internal").ap()
        lo_tab = nc.dram_tensor("lo_tab", (P, DT), BF16, kind="Internal").ap()
        S_tab = nc.dram_tensor("S_tab", (P, SPILL, SW), BF16, kind="Internal").ap()
        dinv_tab = nc.dram_tensor("dinv_tab", (NB * P,), F32, kind="Internal").ap()
        offset_tab = nc.dram_tensor("offset_tab", (P, NT), F32, kind="Internal").ap()

        S = sb("S", [P, NB, SW], BF16)
        U = sb("U", [P, NB * 2 * ROWW // 2], F32)
        agg_sb = sb("agg_sb", [P, 2, CW], F32)
        val = sb("val", [P, CW // P, D], F32)
        xres = sb("xres", [P, CW // P, D], F32)
        parts = sb("parts", [P, CW // P, NPARTS, D], BF16)
        w_sb = sb("w_sb", [P, 2, 2 * D], F32)
        bias_sb = sb("bias_sb", [P, 2 * D], F32)
        dinv = sb("dinv", [P, NB], F32)
        base_i = sb("base_i", [P, NG], I32)
        batch_rel = sb("batch_rel", [P, NDG], I32)
        zero_col = sb("zero_col", [P, 1], F32)
        bn = sb("bn", [P, CW // P, 6], F32)
        mv = sb("mv", [P, CW // P, 2], F32)
        rstd = sb("rstd", [P, CW // P], F32)
        flag_f = sb("flag_f", [P, 12], F32)
        flag_i = sb("flag_i", [P, 1], I32)
        ones = sb("ones", [P, 1], BF16)
        one_f = sb("one_f", [P, 1], F32)
        bias_col = sb("bias_col", [P, 2], F32)
        deg_sb = sb("deg_sb", [P, NB], F32)

        def carve(region, at, shape, dt):
            size = 1
            for s in shape:
                size *= s
            words = -(-size * (2 if dt in (BF16, F16) else 4) // 4)
            view = region[:, at:at + words]
            if dt != F32:
                view = view.bitcast(dt)
            view = view[:, 0:size]
            if len(shape) == 2:
                view = view.rearrange("p (a b) -> p a b", a=shape[0])
            if len(shape) == 3:
                view = view.rearrange("p (a b c) -> p a b c", a=shape[0], b=shape[1])
            return view, at + words

        at = 0
        src_i, at = carve(U, at, [NT], I32)
        dst_i, at = carve(U, at, [NT], I32)
        code_f, at = carve(U, at, [NT], F32)
        lo_f, at = carve(U, at, [NT], BF16)
        off_f, at = carve(U, at, [NT], F32)
        code_iota, at = carve(U, at, [CODES], F16)
        lo_iota, at = carve(U, at, [P], BF16)
        base_f, at = carve(U, at, [NG], F32)
        group_min, at = carve(U, at, [NG], F32)
        ident, at = carve(U, at, [P], BF16)
        code_hot, at = carve(U, at, [2 * GT, CODES], BF16)
        lo_hot, at = carve(U, at, [2, GT, P], BF16)
        window, at = carve(U, at, [2, CODES], BF16)
        assert at <= U.shape[1], at
        U_bf = U[:, :].bitcast(BF16)
        NRING = 4
        at = 0
        acc, at = carve(U, at, [ACW], F32)
        e_w, at = carve(U, at, [NT], F32)
        rows, at = carve(U, at, [NRING, GT, D], F32)
        gather_idx, at = carve(U, at, [NT], U32)
        e_off, at = carve(U, at, [NT], F32)
        win_iota, at = carve(U, at, [WIN], F32)
        hot, at = carve(U, at, [2, GT, WIN], F32)
        hot_w, at = carve(U, at, [2, GT, WIN], F32)
        k_at = U.shape[1] - NJ * D
        assert at <= k_at, at
        S_words = S[:, :, :].rearrange("p h d -> p (h d)").bitcast(F32)
        at = 0
        acc_j, at = carve(S_words, at, [NJ, SW], F32)
        attr, at = carve(S_words, at, [NT, NJ], F32)
        coef0, at = carve(S_words, at, [GT * NJ, WIN], F32)
        coef1, at = carve(S_words, at, [GT * NJ, WIN], F32)
        coef = [coef0, coef1]
        path_w, at = carve(S_words, at, [3, D // 4], F32)
        path_c, at = carve(S_words, at, [NJ, 4], F32)
        K_mat, at = carve(U, k_at, [NJ, D], F32)
        S_start = (NB - SPILL) * SW // 2
        at = S_start
        d_sum0, at = carve(S_words, at, [NB, BW], F32)
        d_sum1, at = carve(S_words, at, [NB, BW], F32)
        d_sum = [d_sum0, d_sum1]
        d_x, at = carve(S_words, at, [NB, D], F32)
        d_code, at = carve(S_words, at, [DT], F32)
        d_lo, at = carve(S_words, at, [DT], BF16)
        d_w, at = carve(S_words, at, [NPARTS, DT], F32)
        d_code_iota, at = carve(S_words, at, [CODES], F16)
        d_lo_iota, at = carve(S_words, at, [P], BF16)
        d_code_hot, at = carve(S_words, at, [2 * GT, CODES], BF16)
        d_lo_hot, at = carve(S_words, at, [NLO, GT, P], BF16)
        d_lo_w, at = carve(S_words, at, [NLO * GT, NPARTS, P], BF16)
        assert at <= S_words.shape[1], at

        at = ACW + NT
        g_src, at = carve(U, at, [NT + NLOOP], U32)
        g_dst_i, at = carve(U, at, [NT + NLOOP], I32)
        g_dst, at = carve(U, at, [NT + NLOOP], F32)
        g_iota, at = carve(U, at, [CW], F32)
        g_hot, at = carve(U, at, [CW], F32)
        g_zero, at = carve(U, at, [CW], BF16)
        g_rows, at = carve(U, at, [2 * ROWW], BF16)
        g_idx, at = carve(U, at, [1], U32)
        assert at <= k_at, at

        pa = ctx.enter_context(nc.psum_tensor("pa", [P, 4, 512], F32))
        pw = ctx.enter_context(nc.psum_tensor("pw", [P, 2, 512], F32))
        pd = ctx.enter_context(nc.psum_tensor("pd", [P, 512], F32))

        s_edges = counter("s_edges")
        s_const = counter("s_const")
        s_zero = counter("s_zero")
        s_prep = counter("s_prep")
        s_pred = counter("s_pred")
        s_code = counter("s_code")
        s_lo = counter("s_lo")
        s_win = counter("s_win")
        s_wcopy = counter("s_wcopy")
        s_wadd = counter("s_wadd")
        s_deg = counter("s_deg")
        s_sqrt = counter("s_sqrt")
        s_dt = counter("s_dt")
        s_dr = counter("s_dr")
        s_bc = counter("s_bc")
        s_tabs = counter("s_tabs")
        s_spill = counter("s_spill")
        s_fill = counter("s_fill")
        s_dload = counter("s_dload")
        s_dprep = counter("s_dprep")
        s_dhot = counter("s_dhot")
        s_dscale = counter("s_dscale")
        s_dwin = counter("s_dwin")
        s_dadd = counter("s_dadd")
        s_dzero = counter("s_dzero")
        s_dmm = counter("s_dmm")
        s_esrc = counter("s_esrc")
        s_off = counter("s_off")
        s_u = [counter(f"s_u{i}") for i in range(5)]
        s_w = counter("s_w")
        s_b = counter("s_b")
        s_agg = counter("s_agg")
        s_aggc = counter("s_aggc")
        s_out = counter("s_out")
        s_v = counter("s_v")
        s_a = counter("s_a")
        s_xl = counter("s_xl")
        s_xs = counter("s_xs")
        s_ps = counter("s_ps")
        s_eload = counter("s_eload")
        s_eload2 = counter("s_eload2")
        s_lane = counter("s_lane")
        s_kmat = counter("s_kmat")
        s_xt = [counter(f"s_xt{i}") for i in range(2)]
        s_accz = counter("s_accz")
        s_rows = [counter(f"s_rows{i}") for i in range(NRING)]
        s_hot = counter("s_hot")
        s_seg = counter("s_seg")
        s_accd = counter("s_accd")
        s_g_load = counter("s_g_load")
        s_g_vec = counter("s_g_vec")
        s_g_pool = counter("s_g_pool")
        s_g_col = counter("s_g_col")
        s_g_rows = []
        s_g_mm = counter("s_g_mm")
        s_g_tick = counter("s_g_tick")
        s_g_done = counter("s_g_done")

        t_dst = sp.run(lambda e: e.dma_start(dst_i, a["dst"][:, 0:NT]), s_edges, 16)
        t_src = act.run(lambda e: e.dma_start(src_i, a["src"][:, 0:NT]), s_esrc, 16)

        def clear(engine, lo, hi):
            return engine.run(lambda e: e.memset(S[:, lo:hi, :].rearrange("p h d -> p (h d)").bitcast(F32), 0.0),
                              s_zero)

        pool.run(lambda e: e.iota(code_iota, pattern=[[1, CODES]], base=0, channel_multiplier=0,
                                  allow_small_or_imprecise_dtypes=True), s_const)
        pool.run(lambda e: e.iota(lo_iota, pattern=[[1, P]], base=0, channel_multiplier=0,
                                  allow_small_or_imprecise_dtypes=True), s_const)
        pool.run(lambda e: e.memset(ones[:, :], 1.0), s_const)
        pool.run(lambda e: e.memset(one_f[:, :], 1.0), s_const)
        pool.run(lambda e: e.memset(zero_col[:, :], 0.0), s_const)
        t_id = pool.run(lambda e: e.memset(ident, 0.0), s_const)
        pool.wait(t_id)
        t_const = pool.run(lambda e: e.affine_select(out=ident, in_=ident, compare_op=ALU.not_equal, fill=1.0,
                                                     base=0, pattern=[[-1, P]], channel_multiplier=1), s_const)
        clear(pool, 0, 12)
        t_clear = clear(dve, 12, NB)

        dve.wait(t_dst)
        t = dve.run(lambda e: e.tensor_copy(off_f, dst_i), s_prep)
        dve.wait(t)
        t = dve.run(lambda e: e.tensor_reduce(group_min, off_f.rearrange("p (g t) -> p g t", t=GT), AX.X, ALU.min),
                    s_prep)
        dve.wait(t)
        t_gmin = dve.run(lambda e: e.tensor_scalar(group_min, group_min, -1.0, None, ALU.mult), s_prep)
        pool.wait(t_gmin)
        t_base = pool.run(lambda e: e.partition_all_reduce(base_f, group_min, P, RMAX), s_pred)
        dve.wait(t_src, t_gmin)
        t_hi = dve.run(lambda e: e.tensor_scalar(dst_i, src_i, 7, None, ALU.arith_shift_right), s_prep)
        dve.wait(t_hi)
        t_code = dve.run(lambda e: e.tensor_copy(code_f, dst_i), s_prep)
        t_lo = dve.run(lambda e: e.tensor_scalar(src_i, src_i, P - 1, None, ALU.bitwise_and), s_prep)
        dve.wait(t_lo)
        t_lof = dve.run(lambda e: e.tensor_copy(lo_f, src_i), s_prep)
        dve.wait(t_base)
        t = dve.run(lambda e: e.tensor_scalar(base_f, base_f, -1.0, None, ALU.mult), s_prep)
        dve.wait(t)
        t_basei = dve.run(lambda e: e.tensor_copy(base_i[:, :], base_f), s_prep)
        first_g = base_f[:, NGG:NG].rearrange("p (b g) -> p b g", g=BG)
        rel = group_min[:, 0:NDG]
        t = dve.run(lambda e: e.tensor_tensor(rel.rearrange("p (b g) -> p b g", g=BG), first_g,
                                              first_g[:, :, 0:1].to_broadcast([P, NDB, BG]), ALU.subtract), s_prep)
        dve.wait(t)
        dve.run(lambda e: e.tensor_copy(batch_rel[:, :], rel), s_prep)
        dve.run(lambda e: e.tensor_reduce(flag_f[:, 7:8], rel, AX.X, ALU.max), s_prep)
        dve.run(lambda e: e.tensor_reduce(flag_f[:, 8:9], rel, AX.X, ALU.min), s_prep)
        off_g = off_f.rearrange("p (g t) -> p g t", t=GT)
        dve.run(lambda e: e.tensor_tensor(off_g, off_g, base_f.unsqueeze(2).to_broadcast([P, NG, GT]), ALU.subtract),
                s_prep)
        beyond = code_hot.rearrange("p a b -> p (a b)").bitcast(F32)[:, 0:NT // 2]
        for h in range(2):
            half = off_f[:, h * (NT // 2):(h + 1) * (NT // 2)]
            dve.wait((s_prep.sem, s_prep.value))
            dve.run(lambda e, half=half: e.tensor_scalar(beyond, half, float(WIN), float(FAR), ALU.is_ge, ALU.mult),
                    s_prep)
            dve.wait((s_prep.sem, s_prep.value))
            t_off = dve.run(lambda e, half=half: e.tensor_tensor(half, half, beyond, ALU.add), s_prep)
        dve.wait(t_off)
        t_codes = dve.run(lambda e: e.scalar_tensor_tensor(out=code_f, in0=code_f, scalar=float(WIN), in1=off_f,
                                                           op0=ALU.mult, op1=ALU.add), s_prep)
        sp.wait(t_off)
        t_offs = sp.run(lambda e: e.dma_start(offset_tab, off_f), s_off, 16)
        sp.wait(t_codes)
        sp.run(lambda e: e.dma_start(code_tab, code_f[:, NGG * GT:NT]), s_tabs, 16)
        t_tabs = sp.run(lambda e: e.dma_start(lo_tab, lo_f[:, NGG * GT:NT]), s_tabs, 16)
        dve.wait(t_const, (s_zero.sem, s_zero.value))
        for h in range(NB):
            n = P if h < NB - 1 else LAST
            t_diag = dve.run(lambda e, h=h, n=n: e.tensor_copy(S[0:n, h, h * P:h * P + n], ident[0:n, 0:n]), s_zero)

        def one_hots(g):
            if g >= 2:
                dve.wait((s_win.sem, g - 1))
            lows = lo_f[:, GT * g:GT * (g + 1)].unsqueeze(2).to_broadcast([P, GT, P])
            lane = lo_iota.unsqueeze(1).to_broadcast([P, GT, P])
            dve.run(lambda e: e.tensor_tensor(lo_hot[:, g % 2], lows, lane, ALU.is_equal), s_lo)
            for t in range(GT):
                col = slice(GT * g + t, GT * g + t + 1)
                dve.run(lambda e, t=t, col=col: e.tensor_scalar(code_hot[:, (g % 2) * GT + t], code_iota,
                                                                code_f[:, col], None, ALU.is_equal), s_code)

        def add_window(g):
            pool.wait((s_wcopy.sem, g + 1))
            if g:
                pool.wait((s_wadd.sem, g))

            def step(e):
                first = e.value_load(base_i[0:1, g:g + 1], min_val=0, max_val=N - 1)
                place = S[:, :, bass.ds(first, WIN)]
                return e.tensor_tensor(place, place, window[:, g % 2].rearrange("p (h w) -> p h w", w=WIN), ALU.add)

            pool.run(step, s_wadd)

        dve.wait(t_codes)
        pool.wait(t_basei, t_diag)
        for g in range(NG):
            b = g % 2
            one_hots(g)
            pe.wait((s_lo.sem, g + 1), (s_code.sem, GT * (g + 1)))
            if g >= 2:
                pe.wait((s_wcopy.sem, g - 1))
            for t in range(GT):
                for bank, (h0, h1) in enumerate(((0, HB), (HB, NB))):
                    last = t == GT - 1 and bank == 1
                    pe.run(lambda e, b=b, t=t, bank=bank, h0=h0, h1=h1: e.matmul(
                        pa[:, 2 * b + bank, 0:(h1 - h0) * WIN], lo_hot[:, b, t],
                        code_hot[:, b * GT + t, h0 * WIN:h1 * WIN], start=(t == 0), stop=(t == GT - 1)),
                        s_win if last else None)
            act.wait((s_win.sem, g + 1))
            if g >= 2:
                act.wait((s_wadd.sem, g - 1))
            act.run(lambda e, b=b: e.activation(window[:, b, 0:HB * WIN], pa[:, 2 * b, 0:HB * WIN], ACT.Copy))
            act.run(lambda e, b=b: e.activation(window[:, b, HB * WIN:CODES], pa[:, 2 * b + 1, 0:CODES - HB * WIN],
                                                ACT.Copy), s_wcopy)
            add_window(g)
        t_S = (s_wadd.sem, NG)
        act.wait(t_S)
        for h in range(NB - SPILL, NB):
            k = h - (NB - SPILL)
            t_spill = act.run(lambda e, h=h, k=k: e.dma_start(S_tab[:, k, :], S[:, h, :]), s_spill, 16)

        pe.wait(t_S, t_const)
        for d in range(NB):
            m = P if d < NB - 1 else LAST
            for h in range(NB):
                k = P if h < NB - 1 else LAST
                last = d == NB - 1 and h == NB - 1
                pe.run(lambda e, d=d, m=m, h=h, k=k: e.matmul(pd[0:m, d:d + 1], S[0:k, h, d * P:d * P + m],
                                                              ones[0:k, :], start=(h == 0), stop=(h == NB - 1)),
                       s_deg if last else None)
        t_deg = (s_deg.sem, 1)
        dve.wait(t_codes)
        t = dve.run(lambda e: e.memset(deg_sb[:, :], 0.0), s_prep)
        dve.wait(t, t_deg)
        dve.run(lambda e: e.tensor_copy(deg_sb[:, 0:NB - 1], pd[:, 0:NB - 1]), s_prep)
        t = dve.run(lambda e: e.tensor_copy(deg_sb[0:LAST, NB - 1:NB], pd[0:LAST, NB - 1:NB]), s_prep)
        dve.wait(t)
        dve.run(lambda e: e.tensor_reduce(flag_f[:, 0:1], deg_sb[:, :], AX.X, ALU.max), s_prep)
        t = dve.run(lambda e: e.tensor_reduce(flag_f[:, 1:2], deg_sb[:, :], AX.X, ALU.add), s_prep)
        pool.wait(t)
        pool.run(lambda e: e.partition_all_reduce(flag_f[:, 2:3], flag_f[:, 0:1], P, RMAX), s_pred)
        t = pool.run(lambda e: e.partition_all_reduce(flag_f[:, 3:4], flag_f[:, 1:2], P, RADD), s_pred)
        dve.wait(t)
        dve.run(lambda e: e.tensor_scalar(flag_f[:, 4:5], flag_f[:, 2:3], float(EXACT), None, ALU.is_ge), s_prep)
        t = dve.run(lambda e: e.tensor_scalar(flag_f[:, 5:6], flag_f[:, 3:4], float(E + N), None, ALU.not_equal),
                    s_prep)
        dve.wait(t)
        dve.run(lambda e: e.tensor_tensor(flag_f[:, 6:7], flag_f[:, 4:5], flag_f[:, 5:6], ALU.max), s_prep)
        dve.run(lambda e: e.tensor_scalar(flag_f[:, 9:10], flag_f[:, 7:8], float(BW - WIN), None, ALU.is_gt), s_prep)
        t = dve.run(lambda e: e.tensor_scalar(flag_f[:, 10:11], flag_f[:, 8:9], 0.0, None, ALU.is_lt), s_prep)
        dve.wait(t)
        t = dve.run(lambda e: e.tensor_tensor(flag_f[:, 9:10], flag_f[:, 9:10], flag_f[:, 10:11], ALU.max), s_prep)
        dve.wait(t)
        t = dve.run(lambda e: e.tensor_tensor(flag_f[:, 6:7], flag_f[:, 6:7], flag_f[:, 9:10], ALU.max), s_prep)
        dve.wait(t)
        t_flag = dve.run(lambda e: e.tensor_copy(flag_i[:, :], flag_f[:, 6:7]), s_prep)

        engines = {"pe": pe, "dve": dve, "act": act, "pool": pool, "sp": sp}

        def load_flag(engine):
            engine.wait(t_flag)

            def step(e):
                engine.general = e.value_load(flag_i[0:1, 0:1], min_val=0, max_val=1)

            engine.run(step)

        for engine in (pe, dve, act, pool, sp):
            load_flag(engine)

        def begin(engine, general):
            def step(e):
                engine.guard = e.If(engine.general > 0) if general else e.If(engine.general < 1)
                engine.guard.__enter__()
            engine.run(step)

        def end(engine):
            def step(e):
                engine.guard.__exit__(None, None, None)
            engine.run(step)

        tiles_done = [0]
        general_bank = [None]

        def general_prepare(u_read):
            begin(sp, True)
            sp.wait(u_read)
            sp.run(lambda e: e.dma_start(g_src, a["src"].bitcast(U32)), s_g_load, 16)
            t = sp.run(lambda e: e.dma_start(g_dst_i, a["dst"]), s_g_load, 16)
            end(sp)
            begin(dve, True)
            dve.wait(u_read, t)
            dve.run(lambda e: e.tensor_copy(g_dst, g_dst_i), s_g_vec)
            end(dve)
            begin(pool, True)
            pool.wait(u_read)
            pool.run(lambda e: e.memset(g_zero, 0.0), s_g_pool)
            end(pool)

        def general_chunk(c, tiles, out, done, table=None, row_at=0, coef=None, ready=None):
            width = chunk_shape(c)[2]
            first = tiles_done[0]
            tiles_done[0] += tiles
            f32 = coef is not None
            hot = (g_hot if f32 else g_hot.bitcast(BF16))[:, 0:width]
            row_len = table.shape[1] if table is not None else 0
            row = (g_rows.bitcast(F32) if f32 else g_rows)[:, 0:row_len]
            if not s_g_rows or s_g_rows[-1].value + 16 * tiles >= 1 << 16:
                s_g_rows.append(counter(f"s_g_rows{len(s_g_rows)}"))
            landed = s_g_rows[-1]
            t_prepared = (s_g_vec.sem, s_g_vec.value)
            t_before = (s_g_done.sem, s_g_done.value) if s_g_done.value else None

            begin(pool, True)
            pool.wait(t_before)
            if table is None:
                pool.run(lambda e: e.memset(g_rows, 1.0), s_g_pool)
            t_iota = pool.run(lambda e: e.iota(g_iota, pattern=[[1, CW]], base=c * CW, channel_multiplier=0,
                                               allow_small_or_imprecise_dtypes=True), s_g_pool)
            if table is not None:
                pool.wait(ready)

                def gather(e):
                    with e.Fori(0, tiles) as i:
                        e.wait_ge(s_g_col.sem, i * 2 + (2 * first + 1))
                        e.sem_inc(s_g_tick.sem, 1)
                        e.indirect_dma_start(row, None, table, bass.IndirectOffsetOnAxis(ap=g_idx, axis=0)) \
                            .then_inc(landed.sem, 16)

                pool.run(gather)
            end(pool)
            rows_first = landed.value
            if table is not None:
                landed.value += 16 * tiles

            def one_hots(e):
                with e.Fori(0, tiles) as i:
                    e.wait_ge(s_g_mm.sem, i + (first + 1))
                    e.tensor_copy(g_idx, g_src[:, bass.ds(i, 1)]).then_inc(s_g_col.sem, 1)
                    if f32:
                        ins = e.tensor_scalar(hot, g_iota[:, 0:width], g_dst[:, bass.ds(i, 1)],
                                              coef(i), ALU.is_equal, ALU.mult)
                    else:
                        ins = e.tensor_scalar(hot, g_iota[:, 0:width], g_dst[:, bass.ds(i, 1)], None, ALU.is_equal)
                    ins.then_inc(s_g_col.sem, 1)

            begin(dve, True)
            dve.wait(t_prepared, t_iota)
            dve.run(one_hots)
            end(dve)

            def products(e):
                if first == 0:
                    e.sem_inc(s_g_mm.sem, 1)
                e.matmul(out, g_zero[:, 0:P], g_zero[:, 0:width], start=True, stop=False, skip_group_check=True)
                with e.Fori(0, tiles) as i:
                    e.wait_ge(s_g_col.sem, i * 2 + (2 * first + 2))
                    if table is not None:
                        e.wait_ge(landed.sem, i * 16 + (rows_first + 16))
                    if f32:
                        ins = e.matmul(out, row, hot, start=False, stop=False, skip_group_check=True)
                    elif table is None:
                        ins = e.matmul(out, g_rows[:, 0:P], hot, start=False, stop=False, skip_group_check=True)
                    else:
                        for part in range(NPARTS):
                            at = row_at + part * D
                            ins = e.matmul(out, row[:, at:at + D], hot, start=False, stop=False,
                                           skip_group_check=True)
                    ins.then_inc(s_g_mm.sem, 1)
                ins = e.matmul(out, g_zero[:, 0:P], g_zero[:, 0:width], start=False, stop=True,
                               skip_group_check=True)
                ins.then_inc(s_g_done.sem, 1)
                if done is not None:
                    e.wait_ge(s_g_done.sem, t_done[1])
                    e.sem_inc(done.sem, 1)

            s_g_done.value += 1
            t_done = (s_g_done.sem, s_g_done.value)
            begin(pe, True)
            pe.wait(t_iota, general_bank[0])
            pe.run(products)
            end(pe)
            return t_done

        general_prepare(t_flag)
        for c in range(NCH):
            nq, m, width = chunk_shape(c)
            t = general_chunk(c, NT + NLOOP, pa[:, 0, 0:width], None)
            begin(dve, True)
            dve.wait(t)
            t = dve.run(lambda e, width=width: e.tensor_copy(g_hot[0:1, 0:width], pa[0:1, 0, 0:width]), s_g_vec)
            end(dve)
            begin(pe, True)
            pe.wait(t)
            for q in range(nq):
                t = pe.run(lambda e, q=q, m=m: e.matmul(pd[0:m, q:q + 1], g_hot[0:1, q * P:q * P + m],
                                                        one_f[0:1, :], start=True, stop=True),
                           s_g_done if q == nq - 1 else None)
            end(pe)
            begin(dve, True)
            dve.wait(t)
            general_bank[0] = dve.run(lambda e, nq=nq, m=m, c=c: e.tensor_copy(
                deg_sb[0:m, c * (CW // P):c * (CW // P) + nq], pd[0:m, 0:nq]), s_g_vec)
            end(dve)
        begin(dve, True)
        dve.wait(general_bank[0])
        end(dve)
        dve.wait(t_flag)
        t = dve.run(lambda e: e.tensor_scalar(dinv[:, :], deg_sb[:, :], 1.0, None, ALU.max), s_prep)
        act.wait(t)
        t = act.run(lambda e: e.activation(dinv[:, :], dinv[:, :], ACT.Sqrt), s_sqrt)
        dve.wait(t)
        t_dinv = dve.run(lambda e: e.reciprocal(dinv[:, :], dinv[:, :]), s_prep)

        sp.wait(t_dinv)
        t_dinv_tab = sp.run(lambda e: e.dma_start(dinv_tab.rearrange("(h p) -> p h", p=P), dinv[:, :],
                                                        allow_slow_non_contiguous=True), s_dt, 16)

        def wait_v(value=None):
            return (s_v.sem, s_v.value)

        state = {
            "unit": 0,
            "out_read": [None, None],
            "agg_free": [None] * 4,
            "agg_sb_read": None,
            "w_read": None,
            "bias_read": None,
            "u_read": t_dinv,
            "bias_col_read": None,
            "S_loaded": None,
            "x_read": None,
            "val_stored": None,
            "parts_stored": None,
        }

        def load_weights(src, nin, nout, bias):
            sp.wait(state["w_read"])
            w = sp.run(lambda e: e.dma_start(w_sb[:, 0:nin, 0:nout * D], src), s_w, 16)
            sp.wait(state["bias_read"])
            b = None
            if bias is not None:
                b = sp.run(lambda e: e.dma_start(bias_sb[:, 0:nout * D], bias), s_b, 16)
            return w, b

        def load_residual(table, c):
            nq, rows_n, n = chunk_shape(c)
            sp.wait(state["x_read"])
            src = table[c * CW:c * CW + n, :].rearrange("(q p) d -> p q d", p=rows_n)
            return sp.run(lambda e: e.dma_start(xres[0:rows_n, 0:nq, :], src), s_xl, 16)

        def dinv_of(c):
            nq, rows_n, _ = chunk_shape(c)
            return dinv[0:rows_n, c * (CW // P):c * (CW // P) + nq].unsqueeze(2).to_broadcast([rows_n, nq, D])

        def split_and_store(c, buf, table, half):
            nq, r, n = chunk_shape(c)
            v = buf[0:r, 0:nq, :]
            part = [parts[0:r, 0:nq, i, :] for i in range(NPARTS)]
            act.wait(wait_v(), state["parts_stored"])
            t0 = act.run(lambda e: e.activation(part[0], v, ACT.Copy), s_a)
            dve.wait(t0)
            t1 = dve.run(lambda e: e.tensor_tensor(v, v, part[0], ALU.subtract), s_v)
            act.wait(t1)
            t2 = act.run(lambda e: e.activation(part[1], v, ACT.Copy), s_a)
            dve.wait(t2)
            t3 = dve.run(lambda e: e.tensor_tensor(part[2], v, part[1], ALU.subtract), s_v)
            sp.wait(t3)
            dest = table[c * CW:c * CW + n, half * ROWW:(half + 1) * ROWW].rearrange("(q p) w -> p q w", p=r)
            state["parts_stored"] = sp.run(
                lambda e: e.dma_start(dest, parts[0:r, 0:nq].rearrange("p q a d -> p q (a d)")), s_ps, 16)

        def layer_norm(c):
            nq, r, _ = chunk_shape(c)
            start = wait_v()
            dve.wait(start)
            for q in range(nq):
                t = dve.run(lambda e, q=q: e.bn_stats(bn[0:r, q, :], val[0:r, q, :]), s_v)
            dve.wait(t)
            for q in range(nq):
                t = dve.run(lambda e, q=q: e.bn_aggr(mv[0:r, q, :], bn[0:r, q, :]), s_v)
            dve.wait(t)
            t = dve.run(lambda e: e.tensor_scalar(rstd[0:r, 0:nq], mv[0:r, 0:nq, 1], LN_EPS, None, ALU.add), s_v)
            act.wait(t)
            t = act.run(lambda e: e.activation(rstd[0:r, 0:nq], rstd[0:r, 0:nq], ACT.Sqrt), s_a)
            dve.wait(t)
            t = dve.run(lambda e: e.reciprocal(rstd[0:r, 0:nq], rstd[0:r, 0:nq]), s_v)
            dve.wait(t)
            for q in range(nq):
                dve.run(lambda e, q=q: e.tensor_scalar(val[0:r, q, :], val[0:r, q, :], mv[0:r, q, 0:1],
                                                       rstd[0:r, q:q + 1], ALU.subtract, ALU.mult), s_v)

        def store_val(c, table):
            nq, r, n = chunk_shape(c)
            sp.wait(wait_v())
            dest = table[c * CW:c * CW + n, :].rearrange("(q p) d -> p q d", p=r)
            state["val_stored"] = sp.run(lambda e: e.dma_start(dest, val[0:r, 0:nq, :]), s_xs, 16)

        def product(c, lhs_of, rhs_of, nin, t_w, wait_for):
            nq, r, _ = chunk_shape(c)
            bank = state["unit"] % 2
            state["unit"] += 1
            pe.wait(t_w, wait_for, state["out_read"][bank])
            for q in range(nq):
                for i in range(nin):
                    last = q == nq - 1 and i == nin - 1
                    lhs, rhs = lhs_of(i, q, r), rhs_of(i)
                    t = pe.run(lambda e, q=q, i=i, lhs=lhs, rhs=rhs: e.matmul(
                        pw[0:r, bank, q * D:(q + 1) * D], lhs, rhs, start=(i == 0), stop=(i == nin - 1)),
                        s_out if last else None)
            return bank, t

        def dstep(fn, *tokens):
            dve.wait(wait_v() if s_v.value else None, *tokens)
            return dve.run(fn, s_v)

        def out_view(c, bank):
            nq, r, _ = chunk_shape(c)
            return pw[0:r, bank, 0:nq * D].rearrange("p (q d) -> p q d", d=D)

        def bias_of(c, half):
            nq, r, _ = chunk_shape(c)
            return bias_sb[0:r, half * D:(half + 1) * D].unsqueeze(1).to_broadcast([r, nq, D])

        def views(c):
            nq, r, _ = chunk_shape(c)
            return val[0:r, 0:nq, :], xres[0:r, 0:nq, :]

        def epilogue_conv(c, half, bank, t_out, t_b, table_out, relu, residual, x_out):
            v, x = views(c)
            out, dv = out_view(c, bank), dinv_of(c)
            state["out_read"][bank] = dstep(lambda e: e.tensor_tensor(v, out, dv, ALU.mult), t_out,
                                            state["val_stored"])
            state["bias_read"] = dstep(lambda e: e.tensor_tensor(v, v, bias_of(c, half), ALU.add), t_b)
            if residual is None:
                dstep(lambda e: e.scalar_tensor_tensor(out=v, in0=v, scalar=0.0, in1=dv, op0=ALU.max, op1=ALU.mult))
                split_and_store(c, val, table_out, half)
                return
            if relu:
                state["x_read"] = dstep(lambda e: e.scalar_tensor_tensor(out=v, in0=v, scalar=0.0, in1=x,
                                                                         op0=ALU.max, op1=ALU.add), residual)
            else:
                state["x_read"] = dstep(lambda e: e.tensor_tensor(v, v, x, ALU.add), residual)
            layer_norm(c)
            store_val(c, x_out)

        def load_parts(table, nhalf):
            view = U_bf[:, 0:NB * nhalf * ROWW].rearrange("p (h w) -> p h w", w=nhalf * ROWW)
            begin(sp, False)
            sp.wait(state["u_read"], state["parts_stored"])
            tokens = []
            per = NB // 5
            for i in range(5):
                full = per if i < 4 else per - 1
                h0 = i * per
                src = table[h0 * P:(h0 + full) * P, 0:nhalf * ROWW].rearrange("(h p) w -> p h w", p=P)
                t = sp.run(lambda e, src=src, h0=h0, full=full: e.dma_start(view[:, h0:h0 + full, :], src),
                           s_u[i], 16)
                if i == 4:
                    tail = table[(NB - 1) * P:N, 0:nhalf * ROWW]
                    t = sp.run(lambda e: e.dma_start(view[0:LAST, NB - 1, :], tail), s_u[i], 16)
                tokens.append(t)
            end(sp)
            return view, tokens, per

        def convolution(table_in, nin, nout, weights, bias, table_out=None, relu=False, x_in=None, x_out=None,
                        next_weights=None):
            fused = next_weights is not None
            t_w, t_b = load_weights(weights, nin, nout, next_weights if fused else bias)
            t_bc = None
            if fused:
                sp.wait(state["bias_col_read"])
                t_bc = sp.run(lambda e: e.dma_start(bias_col[:, :], bias), s_bc, 16)
                next_w = bias_sb[:, :].rearrange("p (i d) -> p i d", d=D)
            general_prepare(state["u_read"])
            view, t_parts, per = load_parts(table_in, nin)
            t_table = state["parts_stored"]
            t_x = [load_residual(x_in, 0) if x_in is not None else None]

            def aggregate(c, i):
                width = chunk_shape(c)[2]
                bank = 2 * (c % 2) + i
                pe.wait(state["agg_free"][bank])
                begin(pe, False)
                for h in range(NB):
                    k = P if h < NB - 1 else LAST
                    if h % per == 0 and c == 0 and i == 0:
                        pe.wait(t_parts[h // per])
                    if h == NB - SPILL and c == 0 and i == 0:
                        pe.wait(state["S_loaded"])
                    for part in range(NPARTS):
                        at = i * ROWW + part * D
                        first, last = h == 0 and part == 0, h == NB - 1 and part == NPARTS - 1
                        t = pe.run(lambda e, h=h, k=k, at=at, first=first, last=last: e.matmul(
                            pa[:, bank, 0:width], view[0:k, h, at:at + D], S[0:k, h, c * CW:c * CW + width],
                            start=first, stop=last), s_agg if last else None)
                end(pe)
                general_bank[0] = None
                general_chunk(c, NT + NLOOP, pa[:, bank, 0:width], s_agg, table_in, row_at=i * ROWW, ready=t_table)
                return t

            def copy_sums(c, i, t_sums):
                width, bank = chunk_shape(c)[2], 2 * (c % 2) + i
                act.wait(t_sums, state["agg_sb_read"])
                t = act.run(lambda e: e.activation(agg_sb[:, i, 0:width], pa[:, bank, 0:width], ACT.Copy), s_aggc)
                state["agg_free"][bank] = t
                return t

            def finish_fused(c, t_copied):
                nq, r, n = chunk_shape(c)
                sp.wait(state["x_read"], t_dinv_tab)
                flat = xres[:, :, :].rearrange("p q d -> p (q d)")
                row = dinv_tab[c * CW:c * CW + n].partition_broadcast(P)
                t_dr = sp.run(lambda e: e.dma_start(flat[:, 0:n], row), s_dr, 16)
                outs = []
                for o in range(2):
                    bank = state["unit"] % 2
                    state["unit"] += 1
                    pe.wait(t_w, t_copied, state["out_read"][bank])
                    for i in range(nin):
                        t = pe.run(lambda e, i=i, o=o, bank=bank: e.matmul(
                            pw[:, bank, 0:n], w_sb[:, i, o * D:(o + 1) * D], agg_sb[:, i, 0:n],
                            start=(i == 0), stop=(i == nin - 1)), s_out if i == nin - 1 else None)
                    outs.append((bank, t))
                state["w_read"] = t
                for o, (bank, _) in enumerate(outs):
                    state["out_read"][bank] = dstep(lambda e, o=o, bank=bank: e.tensor_tensor(
                        agg_sb[:, o, 0:n], pw[:, bank, 0:n], flat[:, 0:n], ALU.mult), t, t_dr)
                    act.wait(state["out_read"][bank], t_bc)
                    t_h = act.run(lambda e, o=o: e.activation(agg_sb[:, o, 0:n], agg_sb[:, o, 0:n], ACT.Relu,
                                                              bias=bias_col[:, o:o + 1]), s_a)
                state["bias_col_read"] = t_h
                state["x_read"] = wait_v()
                bank, t_out = product(c, lambda i, q, r: agg_sb[:, i, q * P:q * P + r],
                                      lambda i: next_w[:, i, :], 2, t_b, t_h)
                state["agg_sb_read"] = t_out
                state["bias_read"] = t_out
                v = views(c)[0]
                out = out_view(c, bank)
                state["out_read"][bank] = dstep(lambda e: e.tensor_tensor(v, out, dinv_of(c), ALU.mult), t_out,
                                                state["val_stored"])
                split_and_store(c, val, table_out, 0)

            def finish(c, t_copied):
                if fused:
                    finish_fused(c, t_copied)
                    return
                for half in range(nout):
                    bank, t_out = product(c, lambda i, q, r: agg_sb[:, i, q * P:q * P + r],
                                          lambda i, half=half: w_sb[:, i, half * D:(half + 1) * D],
                                          nin, t_w, t_copied)
                    state["agg_sb_read"] = state["w_read"] = t_out
                    epilogue_conv(c, half, bank, t_out, t_b, table_out, relu, t_x[0], x_out)
                if x_in is not None and c + 1 < NCH:
                    t_x[0] = load_residual(x_in, c + 1)

            pending = None
            for c in range(NCH):
                t_sums = [aggregate(c, 0)]
                if pending is not None:
                    finish(*pending)
                if nin == 2:
                    t_sums.append(aggregate(c, 1))
                copied = [copy_sums(c, i, t) for i, t in enumerate(t_sums)]
                state["u_read"] = t_sums[-1]
                pending = (c, copied[-1])
            finish(*pending)

        def gate():
            t_w, t_b = load_weights(a["gate_w"], 1, 1, a["gate_b"])
            t_read = [None, None]

            def one_chunk(c):
                n = chunk_shape(c)[2]
                sp.wait(t_read[c % 2])
                t_xt = sp.run(lambda e, c=c, n=n: e.dma_start(agg_sb[:, c % 2, 0:n], a["x_t"][:, c * CW:c * CW + n]),
                              s_xt[c % 2], 16)
                t_x = load_residual(a["x"], c)
                bank, t_out = product(c, lambda i, q, r, c=c: agg_sb[:, c % 2, q * P:q * P + r],
                                      lambda i: w_sb[:, 0, 0:D], 1, t_w, t_xt)
                t_read[c % 2] = state["agg_sb_read"] = state["w_read"] = t_out
                v, x = views(c)
                out = out_view(c, bank)
                state["out_read"][bank] = state["bias_read"] = dstep(
                    lambda e, c=c: e.tensor_tensor(v, out, bias_of(c, 0), ALU.add), t_out, t_b)
                act.wait(wait_v())
                t = act.run(lambda e, v=v: e.activation(v, v, ACT.Sigmoid), s_a)
                state["x_read"] = dstep(lambda e, v=v, x=x: e.tensor_tensor(v, v, x, ALU.mult), t, t_x)
                dstep(lambda e, v=v, c=c: e.tensor_tensor(v, v, dinv_of(c), ALU.mult), t_dinv)
                split_and_store(c, val, narrow_tab[0], 0)

            for c in range(NCH):
                one_chunk(c)

        def gather_groups(groups, table, t_table, coefs, accumulator, ncoef, t_acc, t_edge, between=None):
            rows_read = s_seg.value
            pool.wait(t_edge, t_table)
            dve.wait(t_edge, t_acc)
            width = ncoef * WIN

            def coefficients(g):
                b = g % 2
                if g >= 2:
                    dve.wait((s_seg.sem, rows_read + g - 1))
                off = e_off[:, GT * g:GT * (g + 1)].unsqueeze(2).to_broadcast([P, GT, WIN])
                lane = win_iota.unsqueeze(1).to_broadcast([P, GT, WIN])
                t = dve.run(lambda e: e.tensor_tensor(hot[:, b], off, lane, ALU.is_equal), s_hot)
                dve.wait(t)
                return dve.run(lambda e: coefs(e, g, b), s_hot)

            pe.wait(*state["out_read"])
            t_coef = coefficients(0)
            added = [None, None]
            for g in range(groups):
                slot = g % NRING
                if g >= NRING:
                    pool.wait((s_seg.sem, rows_read + g - NRING + 1))
                for t in range(GT):
                    index = bass.IndirectOffsetOnAxis(ap=gather_idx[:, GT * g + t:GT * g + t + 1], axis=0)
                    t_rows = pool.run(lambda e, slot=slot, t=t, index=index: e.indirect_dma_start(
                        rows[:, slot, t], None, table, index), s_rows[slot], 16)
                pe.wait(t_coef, t_rows, added[g % 2])
                for t in range(GT):
                    rhs = hot_w[:, g % 2, t] if ncoef == 1 else coef[g % 2][:, t * NJ:(t + 1) * NJ, :]
                    t_seg = pe.run(lambda e, g=g, t=t, slot=slot, rhs=rhs: e.matmul(
                        pw[:, g % 2, 0:width], rows[:, slot, t], rhs, start=(t == 0), stop=(t == GT - 1)),
                        s_seg if t == GT - 1 else None)
                if between is not None:
                    between.prepare(g)
                if g + 1 < groups:
                    t_coef = coefficients(g + 1)
                dve.wait(t_seg)
                if s_accd.value:
                    dve.wait((s_accd.sem, s_accd.value))

                def add(e, g=g):
                    first = e.value_load(base_i[0:1, g:g + 1], min_val=0, max_val=N - 1)
                    if ncoef == 1:
                        place = accumulator[:, bass.ds(first, WIN)]
                        return e.tensor_tensor(place, place, pw[:, g % 2, 0:width], ALU.add)
                    place = accumulator[:, :, bass.ds(first, WIN)]
                    sums = pw[:, g % 2, 0:width].rearrange("p (j w) -> p j w", w=WIN)
                    return e.tensor_tensor(place, place, sums, ALU.add)

                added[g % 2] = dve.run(add, s_accd)
                if between is not None:
                    between.finish(g)
            return added[(groups - 1) % 2]

        def dense_half(t_free, t_table, t_ew, t_acc):
            sp.wait(t_free, t_spill, t_tabs)
            act.wait(t_free, t_spill)
            sp.run(lambda e: e.dma_start(d_code, code_tab), s_dload, 16)
            sp.run(lambda e: e.dma_start(d_lo, lo_tab), s_dload, 16)
            sp.wait(t_table)
            full = (NB - 1) * P
            sp.run(lambda e: e.dma_start(d_x[:, 0:NB - 1, :], x_tab[0][0:full, :].rearrange("(h p) d -> p h d", p=P)),
                   s_dload, 16)
            t_load = sp.run(lambda e: e.dma_start(d_x[0:LAST, NB - 1, :], x_tab[0][full:N, :]), s_dload, 16)
            pool.wait(t_free, t_spill)
            pool.run(lambda e: e.iota(d_code_iota, pattern=[[1, CODES]], base=0, channel_multiplier=0,
                                      allow_small_or_imprecise_dtypes=True), s_lane)
            t_iota = pool.run(lambda e: e.iota(d_lo_iota, pattern=[[1, P]], base=0, channel_multiplier=0,
                                               allow_small_or_imprecise_dtypes=True), s_lane)
            w = e_w[:, NGG * GT:NT]
            cut = [d_code_hot.rearrange("p a b -> p (a b)")[:, i * DT:(i + 1) * DT] for i in range(2)]
            dve.wait(t_spill, t_ew)
            t_w = dve.chain(s_dprep, lambda e: e.tensor_copy(cut[0], w),
                            lambda e: e.tensor_copy(d_w[:, 0], cut[0]),
                            lambda e: e.tensor_tensor(d_w[:, 2], w, cut[0], ALU.subtract),
                            lambda e: e.tensor_copy(cut[1], d_w[:, 2]),
                            lambda e: e.tensor_copy(d_w[:, 1], cut[1]),
                            lambda e: e.tensor_tensor(d_w[:, 2], d_w[:, 2], cut[1], ALU.subtract))
            dve.wait(t_w, t_iota, t_load)
            act.wait(t_w)
            pe.wait(*state["agg_free"])
            win0, zero0, mm0, scale0 = s_dwin.value, s_dzero.value, s_dmm.value, s_dscale.value

            def clear(b):
                if b >= 2:
                    act.wait((s_dmm.sem, mm0 + b - 1))
                act.run(lambda e, b=b: e.activation(d_sum[b % 2].rearrange("p h d -> p (h d)"),
                                                    zero_col[:, :].to_broadcast([P, NB * BW]), ACT.Copy), s_dzero)

            def low_one_hots(k):
                b = k % NLO
                if k >= NLO:
                    act.wait((s_dwin.sem, win0 + k - NLO + 1))
                    dve.wait((s_dscale.sem, scale0 + NPARTS * GT * (k - NLO + 1)))
                lows = d_lo[:, GT * k:GT * (k + 1)].unsqueeze(2).to_broadcast([P, GT, P])
                lane = d_lo_iota.unsqueeze(1).to_broadcast([P, GT, P])
                t_low = dve.run(lambda e: e.tensor_tensor(d_lo_hot[:, b], lows, lane, ALU.is_equal), s_dhot)
                act.wait(t_low)
                for t in range(GT):
                    col, slot = GT * k + t, b * GT + t
                    for part in range(NPARTS):
                        t_scaled = act.run(lambda e, t=t, col=col, slot=slot, part=part: e.activation(
                            d_lo_w[:, slot, part], d_lo_hot[:, b, t], ACT.Copy,
                            scale=d_w[:, part, col:col + 1]), s_dscale)
                return t_scaled

            def code_one_hots(k):
                if k >= 2:
                    dve.wait((s_dwin.sem, win0 + k - 1))
                for t in range(GT):
                    col, slot = GT * k + t, (k % 2) * GT + t
                    t_code = dve.run(lambda e, col=col, slot=slot: e.tensor_scalar(
                        d_code_hot[:, slot], d_code_iota, d_code[:, col:col + 1], None, ALU.is_equal), s_dhot)
                return t_code

            lows, codes, adds = {}, {}, {}

            def windows(k):
                b, lo = k % 2, (k % NLO) * GT
                pe.wait(lows[k], codes[k], adds.get(k - 2))
                for t in range(GT):
                    for part in range(NPARTS):
                        for bank, (h0, h1) in enumerate(((0, HB), (HB, NB))):
                            last = t == GT - 1 and part == NPARTS - 1
                            pe.run(lambda e, b=b, lo=lo, t=t, part=part, bank=bank, h0=h0, h1=h1, last=last: e.matmul(
                                pa[:, 2 * b + bank, 0:(h1 - h0) * WIN], d_lo_w[:, lo + t, part],
                                d_code_hot[:, b * GT + t, h0 * WIN:h1 * WIN], start=(t == 0 and part == 0),
                                stop=last), s_dwin if last and bank == 1 else None)

            def add_window(k):
                b, batch = k % 2, k // BG
                dve.wait((s_dwin.sem, win0 + k + 1), (s_dzero.sem, zero0 + batch + 1), adds.get(k - 1))

                def step(e):
                    first = e.value_load(batch_rel[0:1, k:k + 1], min_val=0, max_val=BW - WIN)
                    for bank, (h0, h1) in enumerate(((0, HB), (HB, NB))):
                        place = d_sum[batch % 2][:, h0:h1, bass.ds(first, WIN)]
                        sums = pa[:, 2 * b + bank, 0:(h1 - h0) * WIN].rearrange("p (h w) -> p h w", w=WIN)
                        ins = e.tensor_tensor(place, place, sums, ALU.add)
                    return ins

                adds[k] = dve.run(step, s_dadd)

            def batch_products(b):
                pe.wait(adds[(b + 1) * BG - 1], batch_added[0])
                for h in range(NB):
                    n = P if h < NB - 1 else LAST
                    pe.run(lambda e, h=h, n=n: e.matmul(pd[:, 0:BW], d_x[0:n, h, :], d_sum[b % 2][0:n, h, :],
                                                        start=(h == 0), stop=(h == NB - 1)),
                           s_dmm if h == NB - 1 else None)

            def add_batch(b):
                dve.wait((s_dmm.sem, mm0 + b + 1), (s_accd.sem, s_accd.value))

                def step(e):
                    g = NGG + b * BG
                    first = e.value_load(base_i[0:1, g:g + 1], min_val=0, max_val=N - 1)
                    place = acc[:, bass.ds(first, BW)]
                    return e.tensor_tensor(place, place, pd[:, 0:BW], ALU.add)

                batch_added[0] = dve.run(step, s_accd)

            batch_added = [None]
            pe.wait(t_load)
            clear(0)
            for k in range(NLO - 1):
                lows[k] = low_one_hots(k)
            codes[0] = code_one_hots(0)

            def prepare(i):
                if i < NDG:
                    windows(i)
                    if i % BG == 3 and i // BG + 1 < NDB:
                        clear(i // BG + 1)
                    if i + 1 < NDG:
                        codes[i + 1] = code_one_hots(i + 1)
                    if i + NLO - 1 < NDG:
                        lows[i + NLO - 1] = low_one_hots(i + NLO - 1)

            def finish(i):
                if i < NDG:
                    add_window(i)
                if i >= BG + 1 and (i - 1) % BG == 0 and (i - 1) // BG <= NDB:
                    batch_products((i - 1) // BG - 1)
                    add_batch((i - 1) // BG - 1)

            return Between(prepare, finish)


        def load_edges(t_free):
            sp.wait(t_free, t_offs)
            begin(sp, False)
            sp.run(lambda e: e.dma_start(gather_idx, a["src"][:, 0:NT].bitcast(U32)), s_eload, 16)
            t = sp.run(lambda e: e.dma_start(e_off, offset_tab), s_eload, 16)
            end(sp)
            begin(pool, False)
            pool.wait(t_free)
            t_lane = pool.run(lambda e: e.iota(win_iota, pattern=[[1, WIN]], base=0, channel_multiplier=0,
                                               allow_small_or_imprecise_dtypes=True), s_lane)
            end(pool)
            return t, t_lane

        def weighted():
            t_table = state["val_stored"]
            t_free = state["u_read"]
            t_wt, t_b = load_weights(a["w_l1"], 1, 1, a["b_l1"])
            general_prepare(t_free)
            t_e, t_lane = load_edges(t_free)
            t_ew = sp.run(lambda e: e.dma_start(e_w, a["w"]), s_eload2, 16)
            dve.wait(t_free)
            t_acc = dve.run(lambda e: e.memset(acc, 0.0), s_accz)
            dve.wait(t_ew)
            begin(dve, False)
            dve.wait(t_lane)
            end(dve)

            def coefs(e, g, b):
                w = e_w[:, GT * g:GT * (g + 1)].unsqueeze(2).to_broadcast([P, GT, WIN])
                return e.tensor_tensor(hot_w[:, b], hot[:, b], w, ALU.mult)

            for engine in (pool, dve, pe, act, sp):
                begin(engine, False)
            group = dense_half(t_free, t_table, t_ew, t_acc)
            t_added = gather_groups(NGG, x_tab[0], t_table, coefs, acc, 1, t_acc, t_e, between=group)
            assert NGG >= NDG + 2
            sp.wait((s_dmm.sem, s_dmm.value), (s_dadd.sem, s_dadd.value))
            for h in range(NB - SPILL, NB):
                k = h - (NB - SPILL)
                state["S_loaded"] = sp.run(lambda e, h=h, k=k: e.dma_start(S[:, h, :], S_tab[:, k, :]), s_fill, 16)
            t_added = (s_accd.sem, s_accd.value)
            for engine in (pool, dve, pe, act, sp):
                end(engine)
            for c in range(NCH):
                width = chunk_shape(c)[2]
                t = general_chunk(c, NT, pa[:, 0, 0:width], None, x_tab[0],
                                  coef=lambda i: e_w[:, bass.ds(i, 1)], ready=t_table)
                begin(dve, True)
                dve.wait(t, t_acc)
                general_bank[0] = dve.run(lambda e, c=c, width=width: e.tensor_copy(
                    acc[:, c * CW:c * CW + width], pa[:, 0, 0:width]), s_g_vec)
                end(dve)
            begin(pe, False)
            pe.wait(t_added)
            end(pe)
            begin(pe, True)
            pe.wait(general_bank[0])
            end(pe)
            def one_chunk(c):
                t_x = load_residual(x_tab[0], c)
                bank, t_out = product(c, lambda i, q, r, c=c: acc[:, c * CW + q * P:c * CW + q * P + r],
                                      lambda i: w_sb[:, 0, 0:D], 1, t_wt, t_acc)
                state["w_read"] = state["u_read"] = t_out
                v, x = views(c)
                out = out_view(c, bank)
                state["out_read"][bank] = state["bias_read"] = dstep(
                    lambda e, v=v, out=out, c=c: e.tensor_tensor(v, out, bias_of(c, 0), ALU.add), t_out, t_b,
                    state["val_stored"])
                dstep(lambda e, v=v, x=x: e.tensor_tensor(v, v, x, ALU.add), t_x)
                layer_norm(c)
                store_val(c, x_tab[1])
                dstep(lambda e, v=v, x=x, c=c: e.tensor_tensor(x, v, dinv_of(c), ALU.mult))
                split_and_store(c, xres, narrow_tab[0], 0)
                state["x_read"] = wait_v()

            for c in range(NCH):
                one_chunk(c)

        def tensor_product():
            t_table = state["val_stored"]
            t_free = state["u_read"]
            general_prepare(t_free)
            t_e, t_lane = load_edges(t_free)
            sp.wait(t_free)
            sp.run(lambda e: e.dma_start(attr, a["attr"]), s_eload2, 16)
            sp.run(lambda e: e.dma_start(path_w, a["path_w"]), s_eload2, 16)
            t_attr = sp.run(lambda e: e.dma_start(path_c, a["path_c"]), s_eload2, 16)
            dve.wait(t_free)
            for j in range(NJ):
                t_acc = dve.run(lambda e, j=j: e.memset(acc_j[:, j], 0.0), s_accz)
            dve.wait(t_attr)
            for j in range(NJ):
                dve.run(lambda e, j=j: e.tensor_scalar(K_mat[:, j, 0:32], path_w[:, 0], path_c[:, j, 0:1], None,
                                                       ALU.mult), s_kmat)
                for k in range(3):
                    src = path_w[:, 1 if j < 4 else 2]
                    t_k = dve.run(lambda e, j=j, k=k, src=src: e.tensor_scalar(
                        K_mat[:, j, 32 + k:D:3], src, path_c[:, j, 1 + k:2 + k], None, ALU.mult), s_kmat)
            begin(dve, False)
            dve.wait(t_lane)
            end(dve)

            def coefs(e, g, b):
                h = hot[:, b].unsqueeze(2).to_broadcast([P, GT, NJ, WIN])
                at = attr[:, GT * g:GT * (g + 1), :].unsqueeze(3).to_broadcast([P, GT, NJ, WIN])
                return e.tensor_tensor(coef[b].rearrange("p (t j) w -> p t j w", t=GT), h, at, ALU.mult)

            for engine in (pool, dve, pe):
                begin(engine, False)
            t_added = gather_groups(NG, x_tab[2], t_table, coefs, acc_j, NJ, t_acc, t_e)
            for engine in (pool, dve, pe):
                end(engine)
            attr_flat = attr.rearrange("p t j -> p (t j)")
            for j in range(NJ):
                for c in range(NCH):
                    width = chunk_shape(c)[2]
                    t = general_chunk(c, NT, pa[:, 0, 0:width], None, x_tab[2],
                                      coef=lambda i, j=j: attr_flat[:, bass.ds(i * NJ + j, 1)], ready=t_table)
                    begin(dve, True)
                    dve.wait(t, t_acc)
                    general_bank[0] = dve.run(lambda e, c=c, j=j, width=width: e.tensor_copy(
                        acc_j[:, j, c * CW:c * CW + width], pa[:, 0, 0:width]), s_g_vec)
                    end(dve)
            begin(pe, False)
            pe.wait(t_added)
            end(pe)
            begin(pe, True)
            pe.wait(general_bank[0])
            end(pe)
            def one_chunk(c):
                t_x = load_residual(x_tab[2], c)
                bank, t_out = product(c, lambda j, q, r, c=c: acc_j[:, j, c * CW + q * P:c * CW + q * P + r],
                                      lambda j: K_mat[:, j, :], NJ, t_k, t_acc)
                v, x = views(c)
                out = out_view(c, bank)
                t = dstep(lambda e, v=v, out=out, x=x: e.scalar_tensor_tensor(
                    out=v, in0=out, scalar=NEIGHBORS ** -0.5, in1=x, op0=ALU.mult, op1=ALU.add), t_out, t_x,
                    state["val_stored"])
                state["out_read"][bank] = state["x_read"] = t
                layer_norm(c)
                store_val(c, a["out"])

            for c in range(NCH):
                one_chunk(c)

        gate()
        convolution(narrow_tab[0], 1, 1, a["w_l0_1"], a["b_l0_1"], table_out=narrow_tab[1])
        convolution(narrow_tab[1], 1, 1, a["w_l0_2"], a["b_l0_2"], x_in=a["x"], x_out=x_tab[0])
        weighted()
        convolution(narrow_tab[0], 1, 2, a["w_l2_0"], a["b_l2_0"], table_out=wide_tab[0])
        convolution(wide_tab[0], 2, 2, a["w_l2_1"], a["b_l2_1"], table_out=wide_tab[1])
        convolution(wide_tab[1], 2, 2, a["w_l2_2"], a["b_l2_2"], table_out=narrow_tab[0],
                    next_weights=a["w_l2_3"])
        convolution(narrow_tab[0], 1, 1, a["eye"], a["b_l2_3"], relu=True, x_in=x_tab[1], x_out=x_tab[2])
        tensor_product()
        sp.wait(state["val_stored"])

        block = ctx.enter_context(nc.Block())
        block.sync(sp.emit)
        block.scalar(act.emit)
        block.vector(dve.emit)
        block.gpsimd(pool.emit)
        block.tensor(pe.emit)


def coupling_constants():
    from math import factorial

    import numpy as np

    def cg(j1, m1, j2, m2, j3, m3):
        if m3 != m1 + m2:
            return 0.0
        f = lambda n: factorial(round(n))
        c = ((2.0 * j3 + 1.0) * f(j3 + j1 - j2) * f(j3 - j1 + j2) * f(j1 + j2 - j3) * f(j3 + m3) * f(j3 - m3)
             / (f(j1 + j2 + j3 + 1) * f(j1 - m1) * f(j1 + m1) * f(j2 - m2) * f(j2 + m2))) ** 0.5
        s = 0
        for v in range(max(-j1 + j2 + m3, -j1 + m1, 0), min(j2 + j3 + m1, j3 - j1 + j2, j3 + m3) + 1):
            s += ((-1) ** (v + j2 + m2) * f(j2 + j3 + m1 - v) * f(j1 - m1 + v)
                  / (f(v) * f(j3 - j1 + j2 - v) * f(j3 + m3 - v) * f(v + j1 - j2 - m3)))
        return float(c * s)

    def real_to_complex(l):
        q = np.zeros((2 * l + 1, 2 * l + 1), dtype=np.complex128)
        for m in range(-l, 0):
            q[l + m, l + abs(m)] = 1 / np.sqrt(2)
            q[l + m, l - abs(m)] = -1j / np.sqrt(2)
        q[l, l] = 1
        for m in range(1, l + 1):
            q[l + m, l + abs(m)] = (-1) ** m / np.sqrt(2)
            q[l + m, l - abs(m)] = 1j * (-1) ** m / np.sqrt(2)
        return (-1j) ** l * q

    def wigner(l1, l2, l3):
        c = np.zeros((2 * l1 + 1, 2 * l2 + 1, 2 * l3 + 1))
        for m1 in range(-l1, l1 + 1):
            for m2 in range(-l2, l2 + 1):
                if abs(m1 + m2) <= l3:
                    c[l1 + m1, l2 + m2, l3 + m1 + m2] = cg(l1, m1, l2, m2, l3, m1 + m2)
        r = np.real(np.einsum("ij,kl,mn,ikn->jlm", real_to_complex(l1), real_to_complex(l2),
                              np.conj(real_to_complex(l3).T), c.astype(np.complex128)))
        return r / np.linalg.norm(r)

    mul = D // 4
    to_scalar, to_vector = (1 / (2 * mul)) ** 0.5, (3 / (3 * mul)) ** 0.5
    out = np.zeros((D, NJ, 4))
    comp = np.arange(3 * mul) % 3
    out[:mul, 0, 0] = wigner(0, 0, 0)[0, 0, 0] * to_scalar
    for k in range(3):
        for j in range(3):
            out[:mul, 1 + j, 1 + k] = wigner(0, 1, 1)[0, j, k] * to_vector
        out[mul:, 0, 1 + k] = wigner(1, 0, 1)[comp, 0, k] * to_vector
        out[mul:, 1 + k, 0] = wigner(1, 1, 0)[comp, k, 0] * to_scalar
        for j in range(5):
            out[mul:, 4 + j, 1 + k] = wigner(1, 2, 1)[comp, j, k] * to_vector
    return out.astype(np.float32)


def kernel(**inputs):
    import numpy as np
    import concourse.bacc as bacc
    from concourse.bass_utils import run_bass_kernel_spmd

    v = {k: np.asarray(x) for k, x in inputs.items()}
    src = np.zeros(NT * P, v["src"].dtype)
    dst = np.full(NT * P, FAR, v["dst"].dtype)
    src[:E], dst[:E] = v["src"], v["dst"]
    loop_src = np.zeros(NLOOP * P, v["src"].dtype)
    loop_dst = np.full(NLOOP * P, FAR, v["dst"].dtype)
    loop_src[:N] = loop_dst[:N] = np.arange(N)
    tiles = lambda x: np.ascontiguousarray(x.reshape(-1, P).T)
    w = np.zeros(NT * P, v["edge_weight"].dtype)
    w[:E] = v["edge_weight"]
    attr = np.zeros((NT * P, NJ), v["edge_attr_9"].dtype)
    attr[:E] = v["edge_attr_9"]
    row = lambda b: np.ascontiguousarray(np.broadcast_to(b, (P, b.shape[-1])))
    wide = lambda m: np.ascontiguousarray(m.reshape(-1, P, m.shape[-1]).transpose(1, 0, 2))
    mats = [v[f"L3_gnn_w{i}"][:, 0, :] for i in range(5)]
    stack = lambda s, m: np.concatenate([mats[s], np.repeat(mats[m], 3, axis=0)], axis=0)
    arrays = {
        "x": v["x"], "x_t": np.ascontiguousarray(v["x"].T),
        "src": tiles(np.concatenate([src, loop_src])), "dst": tiles(np.concatenate([dst, loop_dst])),
        "w": tiles(w), "attr": np.ascontiguousarray(attr.reshape(NT, P, NJ).transpose(1, 0, 2)),
        "gate_w": wide(v["L0_gnn_gate_W"]), "gate_b": row(v["L0_gnn_gate_b"]),
        "w_l0_1": wide(v["L0_gnn_W1"]), "b_l0_1": row(v["L0_gnn_b1"]),
        "w_l0_2": wide(v["L0_gnn_W2"]), "b_l0_2": row(v["L0_gnn_b2"]),
        "w_l1": wide(v["L1_gnn_W"].T), "b_l1": row(v["L1_gnn_b"]),
        **{f"w_l2_{i}": wide(v[f"L2_gnn_W{i}"]) for i in range(4)},
        **{f"b_l2_{i}": row(v[f"L2_gnn_b{i}"]) for i in range(4)},
        "b_l2_2": np.ascontiguousarray(v["L2_gnn_b2"].reshape(2, P).T), "eye": wide(np.eye(P, dtype=np.float32)),
        "path_w": np.ascontiguousarray(np.stack([stack(0, 3), stack(1, 2), stack(1, 4)], axis=1)),
        "path_c": coupling_constants(),
    }
    nc = bacc.Bacc("TRN2", target_bir_lowering=False, num_devices=1)
    args = {k: nc.dram_tensor(f"in_{k}", x.shape, mybir.dt.from_np(x.dtype), kind="ExternalInput").ap()
            for k, x in arrays.items()}
    args["out"] = nc.dram_tensor("out", (N, D), F32, kind="ExternalOutput").ap()
    build_program(nc, args)
    r = run_bass_kernel_spmd(nc, [{f"in_{k}": x for k, x in arrays.items()}], core_ids=[0])
    return r.results[0]["out"]
```

```python
from contextlib import ExitStack

import concourse.bass as bass
from concourse import mybir

F32 = mybir.dt.float32
BF16 = mybir.dt.bfloat16
F16 = mybir.dt.float16
I32 = mybir.dt.int32
U32 = mybir.dt.uint32
ALU = mybir.AluOpType
ACT = mybir.ActivationFunctionType
AX = mybir.AxisListType
RMAX = bass.bass_isa.ReduceOp.max
RADD = bass.bass_isa.ReduceOp.add

P = 128
D = 128
N = 3125
E = 100000
NB = -(-N // P)
LAST = N - (NB - 1) * P
CW = 512
NCH = -(-N // CW)
GT = 4
NG = -(-E // (P * GT))
NT = NG * GT
WIN = 22
SW = N + WIN + 1
NLOOP = NB
FAR = 8192
HB = 13
CODES = NB * WIN
EXACT = 256
BG = 8
NDB = NG // 2 // BG
NDG = NDB * BG
NGG = NG - NDG
BW = 152
DT = NDG * GT
NLO = 3
SPILL = 12
PIECES = 5
PER = NB // PIECES
EARLY = range(PIECES - 1)
LATE = 3
CHUNK_DONE = [min((c + 1) * CW * NG // N + LATE, NG - 1) for c in range(NCH)]
NEARLY = sum(g < NG - 1 for g in CHUNK_DONE)
ACW = N + BW + 3
NJ = 9
LN_EPS = 1e-5
NPARTS = 3
ROWW = NPARTS * D
NEIGHBORS = 10.0


class Counter:

    def __init__(self, sem):
        self.sem, self.value = sem, 0


class Engine:

    def __init__(self):
        self.steps = []
        self.guards = []

    def wait(self, *tokens):
        for token in tokens:
            if token is not None:
                self.steps.append(lambda e, t=token: e.wait_ge(t[0], t[1]))

    def run(self, fn, counter=None, by=1):
        if counter is None:
            self.steps.append(fn)
            return None
        counter.value += by
        self.steps.append(lambda e: fn(e).then_inc(counter.sem, by))
        return (counter.sem, counter.value)

    def chain(self, counter, *fns):
        token = None
        for fn in fns:
            self.wait(token)
            token = self.run(fn, counter)
        return token

    def emit(self, engine):
        for step in self.steps:
            step(engine)


class Between:

    def __init__(self, prepare, finish):
        self.prepare, self.finish = prepare, finish


def chunk_shape(c):
    if (c + 1) * CW <= N:
        return CW // P, P, CW
    assert N - c * CW == LAST
    return 1, LAST, LAST


def build_program(nc, a):
    with ExitStack() as ctx:
        def sb(name, shape, dt):
            return ctx.enter_context(nc.sbuf_tensor(name, shape, dt))

        counters = []

        def counter(name):
            counters.append(Counter(ctx.enter_context(nc.semaphore(name))))
            return counters[-1]

        pe, dve, act, pool, sp = Engine(), Engine(), Engine(), Engine(), Engine()

        narrow_tab = [nc.dram_tensor(f"narrow_tab{i}", (N, ROWW), BF16, kind="Internal").ap() for i in range(2)]
        wide_tab = [nc.dram_tensor(f"wide_tab{i}", (N, 2 * ROWW), BF16, kind="Internal").ap() for i in range(2)]
        x_tab = [nc.dram_tensor(f"x_tab{i}", (N, D), F32, kind="Internal").ap() for i in range(3)]
        code_tab = nc.dram_tensor("code_tab", (P, DT), F32, kind="Internal").ap()
        lo_tab = nc.dram_tensor("lo_tab", (P, DT), BF16, kind="Internal").ap()
        S_tab = nc.dram_tensor("S_tab", (P, SPILL, SW), BF16, kind="Internal").ap()
        dinv_tab = nc.dram_tensor("dinv_tab", (NB * P,), F32, kind="Internal").ap()
        offset_tab = nc.dram_tensor("offset_tab", (P, NT), F32, kind="Internal").ap()

        S = sb("S", [P, NB, SW], BF16)
        U = sb("U", [P, NB * 2 * ROWW // 2], F32)
        agg_sb = sb("agg_sb", [P, 2, CW], F32)
        val = sb("val", [P, CW // P, D], F32)
        xres = sb("xres", [P, CW // P, D], F32)
        parts = sb("parts", [P, CW // P, NPARTS, D], BF16)
        w_sb = sb("w_sb", [P, 2, 2 * D], F32)
        bias_sb = sb("bias_sb", [P, 2 * D], F32)
        dinv = sb("dinv", [P, NB], F32)
        base_i = sb("base_i", [P, NG], I32)
        margin = sb("margin", [P, NEARLY], F32)
        batch_rel = sb("batch_rel", [P, NDG], I32)
        zero_col = sb("zero_col", [P, 1], F32)
        bn = sb("bn", [P, CW // P, 6], F32)
        mv = sb("mv", [P, CW // P, 2], F32)
        rstd = sb("rstd", [P, CW // P], F32)
        flag_f = sb("flag_f", [P, 12], F32)
        flag_i = sb("flag_i", [P, 1], I32)
        ones = sb("ones", [P, 1], BF16)
        one_f = sb("one_f", [P, 1], F32)
        bias_col = sb("bias_col", [P, 2], F32)
        deg_sb = sb("deg_sb", [P, NB], F32)

        def carve(region, at, shape, dt):
            size = 1
            for s in shape:
                size *= s
            words = -(-size * (2 if dt in (BF16, F16) else 4) // 4)
            view = region[:, at:at + words]
            if dt != F32:
                view = view.bitcast(dt)
            view = view[:, 0:size]
            if len(shape) == 2:
                view = view.rearrange("p (a b) -> p a b", a=shape[0])
            if len(shape) == 3:
                view = view.rearrange("p (a b c) -> p a b c", a=shape[0], b=shape[1])
            return view, at + words

        at = 0
        src_i, at = carve(U, at, [NT], I32)
        dst_i, at = carve(U, at, [NT], I32)
        code_f, at = carve(U, at, [NT], F32)
        lo_f, at = carve(U, at, [NT], BF16)
        off_f, at = carve(U, at, [NT], F32)
        code_iota, at = carve(U, at, [CODES], F16)
        lo_iota, at = carve(U, at, [P], BF16)
        base_f, at = carve(U, at, [NG], F32)
        group_min, at = carve(U, at, [NG], F32)
        ident, at = carve(U, at, [P], BF16)
        code_hot, at = carve(U, at, [2 * GT, CODES], BF16)
        lo_hot, at = carve(U, at, [2, GT, P], BF16)
        window, at = carve(U, at, [2, CODES], BF16)
        distance, at = carve(U, at, [CODES], F16)
        assert at <= U.shape[1], at
        U_bf = U[:, :].bitcast(BF16)
        NRING = 4
        at = 0
        e_w, at = carve(U, at, [NT], F32)
        g_start = at
        rows, at = carve(U, at, [NRING, GT, D], F32)
        gather_idx, at = carve(U, at, [NT], U32)
        e_off, at = carve(U, at, [NT], F32)
        win_iota, at = carve(U, at, [WIN], F32)
        hot, at = carve(U, at, [2, GT, WIN], F32)
        hot_w, at = carve(U, at, [2, GT, WIN], F32)
        k_at = U.shape[1] - NJ * D
        acc_at = k_at - ACW
        assert max(at, NB * ROWW // 2) <= acc_at, at
        acc, _ = carve(U, acc_at, [ACW], F32)
        S_words = S[:, :, :].rearrange("p h d -> p (h d)").bitcast(F32)
        at = 0
        acc_j, at = carve(S_words, at, [NJ, SW], F32)
        attr, at = carve(S_words, at, [NT, NJ], F32)
        coef0, at = carve(S_words, at, [GT * NJ, WIN], F32)
        coef1, at = carve(S_words, at, [GT * NJ, WIN], F32)
        coef = [coef0, coef1]
        path_w, at = carve(S_words, at, [3, D // 4], F32)
        path_c, at = carve(S_words, at, [NJ, 4], F32)
        K_mat, at = carve(U, k_at, [NJ, D], F32)
        S_start = (NB - SPILL) * SW // 2
        at = S_start
        d_sum0, at = carve(S_words, at, [NB, BW], F32)
        d_sum1, at = carve(S_words, at, [NB, BW], F32)
        d_sum = [d_sum0, d_sum1]
        d_x, at = carve(S_words, at, [NB, D], F32)
        d_code, at = carve(S_words, at, [DT], F32)
        d_lo, at = carve(S_words, at, [DT], BF16)
        d_w, at = carve(S_words, at, [NPARTS, DT], F32)
        d_code_iota, at = carve(S_words, at, [CODES], F16)
        d_lo_iota, at = carve(S_words, at, [P], BF16)
        d_code_hot, at = carve(S_words, at, [2 * GT, CODES], BF16)
        d_lo_hot, at = carve(S_words, at, [NLO, GT, P], BF16)
        d_lo_w, at = carve(S_words, at, [NLO * GT, NPARTS, P], BF16)
        assert at <= S_words.shape[1], at

        at = g_start
        g_src, at = carve(U, at, [NT + NLOOP], U32)
        g_dst_i, at = carve(U, at, [NT + NLOOP], I32)
        g_dst, at = carve(U, at, [NT + NLOOP], F32)
        g_iota, at = carve(U, at, [CW], F32)
        g_hot, at = carve(U, at, [CW], F32)
        g_zero, at = carve(U, at, [CW], BF16)
        g_rows, at = carve(U, at, [2 * ROWW], BF16)
        g_idx, at = carve(U, at, [1], U32)
        assert at <= acc_at, at

        pa = ctx.enter_context(nc.psum_tensor("pa", [P, 4, 512], F32))
        pw = ctx.enter_context(nc.psum_tensor("pw", [P, 2, 512], F32))
        pd = ctx.enter_context(nc.psum_tensor("pd", [P, 512], F32))

        s_edges = counter("s_edges")
        s_const = counter("s_const")
        s_zero = counter("s_zero")
        s_prep = counter("s_prep")
        s_pred = counter("s_pred")
        s_code = counter("s_code")
        s_dist = counter("s_dist")
        s_acode = counter("s_acode")
        s_lo = counter("s_lo")
        s_win = counter("s_win")
        s_wcopy = counter("s_wcopy")
        s_wadd = counter("s_wadd")
        s_deg = counter("s_deg")
        s_sqrt = counter("s_sqrt")
        s_dt = counter("s_dt")
        s_dr = counter("s_dr")
        s_bc = counter("s_bc")
        s_tabs = counter("s_tabs")
        s_spill = counter("s_spill")
        s_fill = counter("s_fill")
        s_dload = counter("s_dload")
        s_dprep = counter("s_dprep")
        s_dhot = counter("s_dhot")
        s_dscale = counter("s_dscale")
        s_dwin = counter("s_dwin")
        s_dadd = counter("s_dadd")
        s_dzero = counter("s_dzero")
        s_dmm = counter("s_dmm")
        s_accza = counter("s_accza")
        s_esrc = counter("s_esrc")
        s_off = counter("s_off")
        s_u = [counter(f"s_u{i}") for i in range(PIECES)]
        s_w = counter("s_w")
        s_b = counter("s_b")
        s_agg = counter("s_agg")
        s_aggc = counter("s_aggc")
        s_out = counter("s_out")
        s_v = counter("s_v")
        s_a = counter("s_a")
        s_xl = counter("s_xl")
        s_ahead = [counter(f"s_ahead{i}") for i in range(2)]
        s_xs = counter("s_xs")
        s_ps = counter("s_ps")
        s_eload = counter("s_eload")
        s_eload2 = counter("s_eload2")
        s_lane = counter("s_lane")
        s_kmat = counter("s_kmat")
        s_xt = [counter(f"s_xt{i}") for i in range(2)]
        s_accz = counter("s_accz")
        s_rows = [counter(f"s_rows{i}") for i in range(NRING)]
        s_hot = counter("s_hot")
        s_seg = counter("s_seg")
        s_accd = counter("s_accd")
        s_g_load = counter("s_g_load")
        s_g_vec = counter("s_g_vec")
        s_g_pool = counter("s_g_pool")
        s_g_col = counter("s_g_col")
        s_g_rows = []
        s_g_mm = counter("s_g_mm")
        s_g_tick = counter("s_g_tick")
        s_g_done = counter("s_g_done")

        t_dst = sp.run(lambda e: e.dma_start(dst_i, a["dst"][:, 0:NT]), s_edges, 16)
        t_src = act.run(lambda e: e.dma_start(src_i, a["src"][:, 0:NT]), s_esrc, 16)

        def clear(engine, lo, hi):
            return engine.run(lambda e: e.memset(S[:, lo:hi, :].rearrange("p h d -> p (h d)").bitcast(F32), 0.0),
                              s_zero)

        pool.run(lambda e: e.iota(code_iota, pattern=[[1, CODES]], base=0, channel_multiplier=0,
                                  allow_small_or_imprecise_dtypes=True), s_const)
        pool.run(lambda e: e.iota(lo_iota, pattern=[[1, P]], base=0, channel_multiplier=0,
                                  allow_small_or_imprecise_dtypes=True), s_const)
        pool.run(lambda e: e.memset(ones[:, :], 1.0), s_const)
        pool.run(lambda e: e.memset(one_f[:, :], 1.0), s_const)
        pool.run(lambda e: e.memset(zero_col[:, :], 0.0), s_const)
        t_id = pool.run(lambda e: e.memset(ident, 0.0), s_const)
        pool.wait(t_id)
        t_const = pool.run(lambda e: e.affine_select(out=ident, in_=ident, compare_op=ALU.not_equal, fill=1.0,
                                                     base=0, pattern=[[-1, P]], channel_multiplier=1), s_const)
        clear(pool, 0, 12)
        t_clear = clear(dve, 12, NB)

        dve.wait(t_dst)
        t = dve.run(lambda e: e.tensor_copy(off_f, dst_i), s_prep)
        dve.wait(t)
        t = dve.run(lambda e: e.tensor_reduce(group_min, off_f.rearrange("p (g t) -> p g t", t=GT), AX.X, ALU.min),
                    s_prep)
        dve.wait(t)
        t_gmin = dve.run(lambda e: e.tensor_scalar(group_min, group_min, -1.0, None, ALU.mult), s_prep)
        pool.wait(t_gmin)
        t_base = pool.run(lambda e: e.partition_all_reduce(base_f, group_min, P, RMAX), s_pred)
        dve.wait(t_src, t_gmin)
        t_hi = dve.run(lambda e: e.tensor_scalar(dst_i, src_i, 7, None, ALU.arith_shift_right), s_prep)
        dve.wait(t_hi)
        t_code = dve.run(lambda e: e.tensor_copy(code_f, dst_i), s_prep)
        t_lo = dve.run(lambda e: e.tensor_scalar(src_i, src_i, P - 1, None, ALU.bitwise_and), s_prep)
        dve.wait(t_lo)
        t_lof = dve.run(lambda e: e.tensor_copy(lo_f, src_i), s_prep)
        dve.wait(t_base)
        t = dve.run(lambda e: e.tensor_scalar(base_f, base_f, -1.0, None, ALU.mult), s_prep)
        dve.wait(t)
        t_basei = dve.run(lambda e: e.tensor_copy(base_i[:, :], base_f), s_prep)
        for c in range(NEARLY):
            dve.run(lambda e, c=c: e.tensor_reduce(margin[:, c:c + 1], base_f[:, CHUNK_DONE[c] + 1:NG], AX.X, ALU.min),
                    s_prep)
            dve.wait((s_prep.sem, s_prep.value))
            dve.run(lambda e, c=c: e.tensor_scalar(margin[:, c:c + 1], margin[:, c:c + 1], float((c + 1) * CW), None,
                                                   ALU.subtract), s_prep)
        first_g = base_f[:, NGG:NG].rearrange("p (b g) -> p b g", g=BG)
        rel = group_min[:, 0:NDG]
        t = dve.run(lambda e: e.tensor_tensor(rel.rearrange("p (b g) -> p b g", g=BG), first_g,
                                              first_g[:, :, 0:1].to_broadcast([P, NDB, BG]), ALU.subtract), s_prep)
        dve.wait(t)
        dve.run(lambda e: e.tensor_copy(batch_rel[:, :], rel), s_prep)
        dve.run(lambda e: e.tensor_reduce(flag_f[:, 7:8], rel, AX.X, ALU.max), s_prep)
        dve.run(lambda e: e.tensor_reduce(flag_f[:, 8:9], rel, AX.X, ALU.min), s_prep)
        off_g = off_f.rearrange("p (g t) -> p g t", t=GT)
        dve.run(lambda e: e.tensor_tensor(off_g, off_g, base_f.unsqueeze(2).to_broadcast([P, NG, GT]), ALU.subtract),
                s_prep)
        beyond = code_hot.rearrange("p a b -> p (a b)").bitcast(F32)[:, 0:NT // 2]
        for h in range(2):
            half = off_f[:, h * (NT // 2):(h + 1) * (NT // 2)]
            dve.wait((s_prep.sem, s_prep.value))
            dve.run(lambda e, half=half: e.tensor_scalar(beyond, half, float(WIN), float(FAR), ALU.is_ge, ALU.mult),
                    s_prep)
            dve.wait((s_prep.sem, s_prep.value))
            t_off = dve.run(lambda e, half=half: e.tensor_tensor(half, half, beyond, ALU.add), s_prep)
        dve.wait(t_off)
        t_codes = dve.run(lambda e: e.scalar_tensor_tensor(out=code_f, in0=code_f, scalar=float(WIN), in1=off_f,
                                                           op0=ALU.mult, op1=ALU.add), s_prep)
        sp.wait(t_off)
        t_offs = sp.run(lambda e: e.dma_start(offset_tab, off_f), s_off, 16)
        sp.wait(t_codes)
        sp.run(lambda e: e.dma_start(code_tab, code_f[:, NGG * GT:NT]), s_tabs, 16)
        t_tabs = sp.run(lambda e: e.dma_start(lo_tab, lo_f[:, NGG * GT:NT]), s_tabs, 16)
        dve.wait(t_const, (s_zero.sem, s_zero.value))
        for h in range(NB):
            n = P if h < NB - 1 else LAST
            t_diag = dve.run(lambda e, h=h, n=n: e.tensor_copy(S[0:n, h, h * P:h * P + n], ident[0:n, 0:n]), s_zero)

        def one_hots(g):
            if g >= 2:
                dve.wait((s_win.sem, g - 1))
            lows = lo_f[:, GT * g:GT * (g + 1)].unsqueeze(2).to_broadcast([P, GT, P])
            lane = lo_iota.unsqueeze(1).to_broadcast([P, GT, P])
            dve.run(lambda e: e.tensor_tensor(lo_hot[:, g % 2], lows, lane, ALU.is_equal), s_lo)
            for t in range(GT - g % 2):
                col = slice(GT * g + t, GT * g + t + 1)
                dve.run(lambda e, t=t, col=col: e.tensor_scalar(code_hot[:, (g % 2) * GT + t], code_iota,
                                                                code_f[:, col], None, ALU.is_equal), s_code)

        def last_one_hot(g):
            b, col = g % 2, GT * g + GT - 1
            if g >= 2:
                act.wait((s_win.sem, g - 1), (s_acode.sem, g // 2))
            t = act.run(lambda e: e.activation(distance, code_iota, ACT.Abs, scale=-1.0,
                                               bias=code_f[:, col:col + 1]), s_dist)
            act.wait(t)
            act.run(lambda e: e.activation(code_hot[:, b * GT + GT - 1], distance, ACT.Relu, scale=-1.0,
                                           bias=one_f[:, :]), s_acode)

        def add_window(g):
            first = []

            def read_base(e):
                first.append(e.value_load(base_i[0:1, g:g + 1], min_val=0, max_val=N - 1))

            def step(e):
                place = S[:, :, bass.ds(first[0], WIN)]
                return e.tensor_tensor(place, place, window[:, g % 2].rearrange("p (h w) -> p h w", w=WIN), ALU.add)

            pool.run(read_base)
            pool.wait((s_wcopy.sem, g + 1))
            if g:
                pool.wait((s_wadd.sem, g))
            pool.run(step, s_wadd)

        dve.wait(t_codes)
        act.wait(t_codes, t_const)
        pool.wait(t_basei, t_diag)
        last_one_hot(1)
        for g in range(NG):
            b = g % 2
            one_hots(g)
            pe.wait((s_lo.sem, g + 1), (s_code.sem, GT * (g + 1) - (g + 1) // 2), (s_acode.sem, (g + 1) // 2))
            if g >= 2:
                pe.wait((s_wcopy.sem, g - 1))
            for t in range(GT):
                for bank, (h0, h1) in enumerate(((0, HB), (HB, NB))):
                    last = t == GT - 1 and bank == 1
                    pe.run(lambda e, b=b, t=t, bank=bank, h0=h0, h1=h1: e.matmul(
                        pa[:, 2 * b + bank, 0:(h1 - h0) * WIN], lo_hot[:, b, t],
                        code_hot[:, b * GT + t, h0 * WIN:h1 * WIN], start=(t == 0), stop=(t == GT - 1)),
                        s_win if last else None)
            act.wait((s_win.sem, g + 1))
            if g >= 2:
                act.wait((s_wadd.sem, g - 1))
            act.run(lambda e, b=b: e.activation(window[:, b, 0:HB * WIN], pa[:, 2 * b, 0:HB * WIN], ACT.Copy))
            act.run(lambda e, b=b: e.activation(window[:, b, HB * WIN:CODES], pa[:, 2 * b + 1, 0:CODES - HB * WIN],
                                                ACT.Copy), s_wcopy)
            if g % 2 == 1 and g + 2 < NG:
                last_one_hot(g + 2)
            add_window(g)
        t_S = (s_wadd.sem, NG)

        pe.wait(t_S, t_const)
        for d in range(NB):
            m = P if d < NB - 1 else LAST
            for h in range(NB):
                k = P if h < NB - 1 else LAST
                last = d == NB - 1 and h == NB - 1
                pe.run(lambda e, d=d, m=m, h=h, k=k: e.matmul(pd[0:m, d:d + 1], S[0:k, h, d * P:d * P + m],
                                                              ones[0:k, :], start=(h == 0), stop=(h == NB - 1)),
                       s_deg if last else None)
        t_deg = (s_deg.sem, 1)
        dve.wait(t_codes)
        t = dve.run(lambda e: e.memset(deg_sb[:, :], 0.0), s_prep)
        dve.wait(t, t_deg)
        dve.run(lambda e: e.tensor_copy(deg_sb[:, 0:NB - 1], pd[:, 0:NB - 1]), s_prep)
        t = dve.run(lambda e: e.tensor_copy(deg_sb[0:LAST, NB - 1:NB], pd[0:LAST, NB - 1:NB]), s_prep)
        dve.wait(t)
        dve.run(lambda e: e.tensor_reduce(flag_f[:, 0:1], deg_sb[:, :], AX.X, ALU.max), s_prep)
        dve.run(lambda e: e.tensor_reduce(flag_f[:, 11:12], margin[:, :], AX.X, ALU.min), s_prep)
        t = dve.run(lambda e: e.tensor_reduce(flag_f[:, 1:2], deg_sb[:, :], AX.X, ALU.add), s_prep)
        pool.wait(t)
        pool.run(lambda e: e.partition_all_reduce(flag_f[:, 2:3], flag_f[:, 0:1], P, RMAX), s_pred)
        t = pool.run(lambda e: e.partition_all_reduce(flag_f[:, 3:4], flag_f[:, 1:2], P, RADD), s_pred)
        dve.wait(t)
        dve.run(lambda e: e.tensor_scalar(flag_f[:, 4:5], flag_f[:, 2:3], float(EXACT), None, ALU.is_ge), s_prep)
        t = dve.run(lambda e: e.tensor_scalar(flag_f[:, 5:6], flag_f[:, 3:4], float(E + N), None, ALU.not_equal),
                    s_prep)
        dve.wait(t)
        dve.run(lambda e: e.tensor_tensor(flag_f[:, 6:7], flag_f[:, 4:5], flag_f[:, 5:6], ALU.max), s_prep)
        dve.run(lambda e: e.tensor_scalar(flag_f[:, 9:10], flag_f[:, 7:8], float(BW - WIN), None, ALU.is_gt), s_prep)
        dve.run(lambda e: e.tensor_tensor(flag_f[:, 8:9], flag_f[:, 8:9], flag_f[:, 11:12], ALU.min), s_prep)
        dve.wait((s_prep.sem, s_prep.value))
        t = dve.run(lambda e: e.tensor_scalar(flag_f[:, 10:11], flag_f[:, 8:9], 0.0, None, ALU.is_lt), s_prep)
        dve.wait(t)
        t = dve.run(lambda e: e.tensor_tensor(flag_f[:, 9:10], flag_f[:, 9:10], flag_f[:, 10:11], ALU.max), s_prep)
        dve.wait(t)
        t = dve.run(lambda e: e.tensor_tensor(flag_f[:, 6:7], flag_f[:, 6:7], flag_f[:, 9:10], ALU.max), s_prep)
        dve.wait(t)
        t_flag = dve.run(lambda e: e.tensor_copy(flag_i[:, :], flag_f[:, 6:7]), s_prep)

        engines = {"pe": pe, "dve": dve, "act": act, "pool": pool, "sp": sp}

        def load_flag(engine):
            engine.wait(t_flag, t_offs, t_tabs)

            def step(e):
                engine.general = e.value_load(flag_i[0:1, 0:1], min_val=0, max_val=1)

            engine.run(step)

        for engine in (pe, dve, act, pool, sp):
            load_flag(engine)

        def begin(engine, general):
            def step(e):
                guard = e.If(engine.general > 0) if general else e.If(engine.general < 1)
                guard.__enter__()
                engine.guards.append(guard)
            engine.run(step)

        def end(engine):
            def step(e):
                engine.guards.pop().__exit__(None, None, None)
            engine.run(step)

        tiles_done = [0]
        general_bank = [None]

        def general_prepare(u_read):
            begin(sp, True)
            sp.wait(u_read)
            sp.run(lambda e: e.dma_start(g_src, a["src"].bitcast(U32)), s_g_load, 16)
            t = sp.run(lambda e: e.dma_start(g_dst_i, a["dst"]), s_g_load, 16)
            end(sp)
            begin(dve, True)
            dve.wait(u_read, t)
            dve.run(lambda e: e.tensor_copy(g_dst, g_dst_i), s_g_vec)
            end(dve)
            begin(pool, True)
            pool.wait(u_read)
            pool.run(lambda e: e.memset(g_zero, 0.0), s_g_pool)
            end(pool)

        def general_chunk(c, tiles, out, done, table=None, row_at=0, coef=None, ready=None):
            width = chunk_shape(c)[2]
            first = tiles_done[0]
            tiles_done[0] += tiles
            f32 = coef is not None
            hot = (g_hot if f32 else g_hot.bitcast(BF16))[:, 0:width]
            row_len = table.shape[1] if table is not None else 0
            row = (g_rows.bitcast(F32) if f32 else g_rows)[:, 0:row_len]
            if not s_g_rows or s_g_rows[-1].value + 16 * tiles >= 1 << 16:
                s_g_rows.append(counter(f"s_g_rows{len(s_g_rows)}"))
            landed = s_g_rows[-1]
            t_prepared = (s_g_vec.sem, s_g_vec.value)
            t_before = (s_g_done.sem, s_g_done.value) if s_g_done.value else None

            begin(pool, True)
            pool.wait(t_before)
            if table is None:
                pool.run(lambda e: e.memset(g_rows, 1.0), s_g_pool)
            t_iota = pool.run(lambda e: e.iota(g_iota, pattern=[[1, CW]], base=c * CW, channel_multiplier=0,
                                               allow_small_or_imprecise_dtypes=True), s_g_pool)
            if table is not None:
                pool.wait(ready)

                def gather(e):
                    with e.Fori(0, tiles) as i:
                        e.wait_ge(s_g_col.sem, i * 2 + (2 * first + 1))
                        e.sem_inc(s_g_tick.sem, 1)
                        e.indirect_dma_start(row, None, table, bass.IndirectOffsetOnAxis(ap=g_idx, axis=0)) \
                            .then_inc(landed.sem, 16)

                pool.run(gather)
            end(pool)
            rows_first = landed.value
            if table is not None:
                landed.value += 16 * tiles

            def one_hots(e):
                with e.Fori(0, tiles) as i:
                    e.wait_ge(s_g_mm.sem, i + (first + 1))
                    e.tensor_copy(g_idx, g_src[:, bass.ds(i, 1)]).then_inc(s_g_col.sem, 1)
                    if f32:
                        ins = e.tensor_scalar(hot, g_iota[:, 0:width], g_dst[:, bass.ds(i, 1)],
                                              coef(i), ALU.is_equal, ALU.mult)
                    else:
                        ins = e.tensor_scalar(hot, g_iota[:, 0:width], g_dst[:, bass.ds(i, 1)], None, ALU.is_equal)
                    ins.then_inc(s_g_col.sem, 1)

            begin(dve, True)
            dve.wait(t_prepared, t_iota)
            dve.run(one_hots)
            end(dve)

            def products(e):
                if first == 0:
                    e.sem_inc(s_g_mm.sem, 1)
                e.matmul(out, g_zero[:, 0:P], g_zero[:, 0:width], start=True, stop=False, skip_group_check=True)
                with e.Fori(0, tiles) as i:
                    e.wait_ge(s_g_col.sem, i * 2 + (2 * first + 2))
                    if table is not None:
                        e.wait_ge(landed.sem, i * 16 + (rows_first + 16))
                    if f32:
                        ins = e.matmul(out, row, hot, start=False, stop=False, skip_group_check=True)
                    elif table is None:
                        ins = e.matmul(out, g_rows[:, 0:P], hot, start=False, stop=False, skip_group_check=True)
                    else:
                        for part in range(NPARTS):
                            at = row_at + part * D
                            ins = e.matmul(out, row[:, at:at + D], hot, start=False, stop=False,
                                           skip_group_check=True)
                    ins.then_inc(s_g_mm.sem, 1)
                ins = e.matmul(out, g_zero[:, 0:P], g_zero[:, 0:width], start=False, stop=True,
                               skip_group_check=True)
                ins.then_inc(s_g_done.sem, 1)
                if done is not None:
                    e.wait_ge(s_g_done.sem, t_done[1])
                    e.sem_inc(done.sem, 1)

            s_g_done.value += 1
            t_done = (s_g_done.sem, s_g_done.value)
            begin(pe, True)
            pe.wait(t_iota, general_bank[0])
            pe.run(products)
            end(pe)
            return t_done

        general_prepare(t_flag)
        for engine in (pe, dve, pool):
            begin(engine, True)
        for c in range(NCH):
            nq, m, width = chunk_shape(c)
            t = general_chunk(c, NT + NLOOP, pa[:, 0, 0:width], None)
            begin(dve, True)
            dve.wait(t)
            t = dve.run(lambda e, width=width: e.tensor_copy(g_hot[0:1, 0:width], pa[0:1, 0, 0:width]), s_g_vec)
            end(dve)
            begin(pe, True)
            pe.wait(t)
            for q in range(nq):
                t = pe.run(lambda e, q=q, m=m: e.matmul(pd[0:m, q:q + 1], g_hot[0:1, q * P:q * P + m],
                                                        one_f[0:1, :], start=True, stop=True),
                           s_g_done if q == nq - 1 else None)
            end(pe)
            begin(dve, True)
            dve.wait(t)
            general_bank[0] = dve.run(lambda e, nq=nq, m=m, c=c: e.tensor_copy(
                deg_sb[0:m, c * (CW // P):c * (CW // P) + nq], pd[0:m, 0:nq]), s_g_vec)
            end(dve)
        for engine in (pe, dve, pool):
            end(engine)
        begin(dve, True)
        dve.wait(general_bank[0])
        end(dve)
        dve.wait(t_flag)
        t = dve.run(lambda e: e.tensor_scalar(dinv[:, :], deg_sb[:, :], 1.0, None, ALU.max), s_prep)
        act.wait(t)
        t = act.run(lambda e: e.activation(dinv[:, :], dinv[:, :], ACT.Sqrt), s_sqrt)
        dve.wait(t)
        t_dinv = dve.run(lambda e: e.reciprocal(dinv[:, :], dinv[:, :]), s_prep)

        sp.wait(t_dinv)
        t_dinv_tab = sp.run(lambda e: e.dma_start(dinv_tab.rearrange("(h p) -> p h", p=P), dinv[:, :],
                                                        allow_slow_non_contiguous=True), s_dt, 16)

        def wait_v(value=None):
            return (s_v.sem, s_v.value)

        state = {
            "unit": 0,
            "out_read": [None, None],
            "agg_free": [None] * 4,
            "agg_sb_read": None,
            "w_read": None,
            "bias_read": None,
            "u_read": t_dinv,
            "bias_col_read": None,
            "S_loaded": None,
            "x_read": None,
            "ahead_read": [None, None],
            "val_stored": None,
            "parts_stored": None,
            "pieces": [None] * PIECES,
        }

        def load_weights(src, nin, nout, bias):
            sp.wait(state["w_read"])
            w = sp.run(lambda e: e.dma_start(w_sb[:, 0:nin, 0:nout * D], src), s_w, 16)
            sp.wait(state["bias_read"])
            b = None
            if bias is not None:
                b = sp.run(lambda e: e.dma_start(bias_sb[:, 0:nout * D], bias), s_b, 16)
            return w, b

        def load_residual(table, c):
            nq, rows_n, n = chunk_shape(c)
            sp.wait(state["x_read"])
            src = table[c * CW:c * CW + n, :].rearrange("(q p) d -> p q d", p=rows_n)
            return sp.run(lambda e: e.dma_start(xres[0:rows_n, 0:nq, :], src), s_xl, 16)

        def ahead_view(c):
            nq, rows_n, _ = chunk_shape(c)
            return agg_sb[0:rows_n, c % 2, 0:nq * D].rearrange("p (q d) -> p q d", d=D)

        def load_ahead(table, c):
            nq, rows_n, n = chunk_shape(c)
            sp.wait(state["agg_sb_read"], state["ahead_read"][c % 2])
            src = table[c * CW:c * CW + n, :].rearrange("(q p) d -> p q d", p=rows_n)
            return sp.run(lambda e: e.dma_start(ahead_view(c), src), s_ahead[c % 2], 16)

        def dinv_of(c):
            nq, rows_n, _ = chunk_shape(c)
            return dinv[0:rows_n, c * (CW // P):c * (CW // P) + nq].unsqueeze(2).to_broadcast([rows_n, nq, D])

        def split_and_store(c, buf, table, half):
            nq, r, n = chunk_shape(c)
            v = buf[0:r, 0:nq, :]
            part = [parts[0:r, 0:nq, i, :] for i in range(NPARTS)]
            act.wait(wait_v(), state["parts_stored"])
            t0 = act.run(lambda e: e.activation(part[0], v, ACT.Copy), s_a)
            dve.wait(t0)
            t1 = dve.run(lambda e: e.tensor_tensor(v, v, part[0], ALU.subtract), s_v)
            act.wait(t1)
            t2 = act.run(lambda e: e.activation(part[1], v, ACT.Copy), s_a)
            dve.wait(t2)
            t3 = dve.run(lambda e: e.tensor_tensor(part[2], v, part[1], ALU.subtract), s_v)
            sp.wait(t3)
            dest = table[c * CW:c * CW + n, half * ROWW:(half + 1) * ROWW].rearrange("(q p) w -> p q w", p=r)
            state["parts_stored"] = sp.run(
                lambda e: e.dma_start(dest, parts[0:r, 0:nq].rearrange("p q a d -> p q (a d)")), s_ps, 16)

        def layer_norm(c):
            nq, r, _ = chunk_shape(c)
            start = wait_v()
            dve.wait(start)
            for q in range(nq):
                t = dve.run(lambda e, q=q: e.bn_stats(bn[0:r, q, :], val[0:r, q, :]), s_v)
            dve.wait(t)
            for q in range(nq):
                t = dve.run(lambda e, q=q: e.bn_aggr(mv[0:r, q, :], bn[0:r, q, :]), s_v)
            dve.wait(t)
            t = dve.run(lambda e: e.tensor_scalar(rstd[0:r, 0:nq], mv[0:r, 0:nq, 1], LN_EPS, None, ALU.add), s_v)
            act.wait(t)
            t = act.run(lambda e: e.activation(rstd[0:r, 0:nq], rstd[0:r, 0:nq], ACT.Sqrt), s_a)
            dve.wait(t)
            t = dve.run(lambda e: e.reciprocal(rstd[0:r, 0:nq], rstd[0:r, 0:nq]), s_v)
            dve.wait(t)
            for q in range(nq):
                dve.run(lambda e, q=q: e.tensor_scalar(val[0:r, q, :], val[0:r, q, :], mv[0:r, q, 0:1],
                                                       rstd[0:r, q:q + 1], ALU.subtract, ALU.mult), s_v)

        def store_val(c, table):
            nq, r, n = chunk_shape(c)
            sp.wait(wait_v())
            dest = table[c * CW:c * CW + n, :].rearrange("(q p) d -> p q d", p=r)
            state["val_stored"] = sp.run(lambda e: e.dma_start(dest, val[0:r, 0:nq, :]), s_xs, 16)

        def product(c, lhs_of, rhs_of, nin, t_w, wait_for, psum=pw):
            nq, r, _ = chunk_shape(c)
            bank = state["unit"] % 2
            state["unit"] += 1
            pe.wait(t_w, wait_for, state["out_read"][bank])
            for q in range(nq):
                for i in range(nin):
                    last = q == nq - 1 and i == nin - 1
                    lhs, rhs = lhs_of(i, q, r), rhs_of(i)
                    t = pe.run(lambda e, q=q, i=i, lhs=lhs, rhs=rhs: e.matmul(
                        psum[0:r, bank, q * D:(q + 1) * D], lhs, rhs, start=(i == 0), stop=(i == nin - 1)),
                        s_out if last else None)
            return bank, t

        def dstep(fn, *tokens):
            dve.wait(wait_v() if s_v.value else None, *tokens)
            return dve.run(fn, s_v)

        def out_view(c, bank, psum=pw):
            nq, r, _ = chunk_shape(c)
            return psum[0:r, bank, 0:nq * D].rearrange("p (q d) -> p q d", d=D)

        def bias_of(c, half):
            nq, r, _ = chunk_shape(c)
            return bias_sb[0:r, half * D:(half + 1) * D].unsqueeze(1).to_broadcast([r, nq, D])

        def views(c):
            nq, r, _ = chunk_shape(c)
            return val[0:r, 0:nq, :], xres[0:r, 0:nq, :]

        def epilogue_conv(c, half, bank, t_out, t_b, table_out, relu, residual, x_out):
            v, x = views(c)
            out, dv = out_view(c, bank), dinv_of(c)
            state["out_read"][bank] = dstep(lambda e: e.tensor_tensor(v, out, dv, ALU.mult), t_out,
                                            state["val_stored"])
            state["bias_read"] = dstep(lambda e: e.tensor_tensor(v, v, bias_of(c, half), ALU.add), t_b)
            if residual is None:
                dstep(lambda e: e.scalar_tensor_tensor(out=v, in0=v, scalar=0.0, in1=dv, op0=ALU.max, op1=ALU.mult))
                split_and_store(c, val, table_out, half)
                return
            if relu:
                state["x_read"] = dstep(lambda e: e.scalar_tensor_tensor(out=v, in0=v, scalar=0.0, in1=x,
                                                                         op0=ALU.max, op1=ALU.add), residual)
            else:
                state["x_read"] = dstep(lambda e: e.tensor_tensor(v, v, x, ALU.add), residual)
            layer_norm(c)
            store_val(c, x_out)

        def load_pieces(table, nhalf, pieces, *ready):
            view = U_bf[:, 0:NB * nhalf * ROWW].rearrange("p (h w) -> p h w", w=nhalf * ROWW)
            begin(sp, False)
            sp.wait(*ready)
            for i in pieces:
                full = PER if i < PIECES - 1 else PER - 1
                h0 = i * PER
                src = table[h0 * P:(h0 + full) * P, 0:nhalf * ROWW].rearrange("(h p) w -> p h w", p=P)
                t = sp.run(lambda e, src=src, h0=h0, full=full: e.dma_start(view[:, h0:h0 + full, :], src),
                           s_u[i], 16)
                if i == PIECES - 1:
                    tail = table[(NB - 1) * P:N, 0:nhalf * ROWW]
                    t = sp.run(lambda e: e.dma_start(view[0:LAST, NB - 1, :], tail), s_u[i], 16)
                state["pieces"][i] = t
            end(sp)
            return view

        def load_early(c, stored):
            if c == NCH - 3:
                load_pieces(narrow_tab[0], 1, EARLY[:-1], state["u_read"], stored)
            if c == NCH - 2:
                load_pieces(narrow_tab[0], 1, EARLY[-1:], stored)

        def convolution(table_in, nin, nout, weights, bias, table_out=None, relu=False, x_in=None, x_out=None,
                        next_weights=None, next_nin=0, after_loads=None):
            fused = next_weights is not None
            t_w, t_b = load_weights(weights, nin, nout, next_weights if fused else bias)
            t_bc = None
            if fused:
                sp.wait(state["bias_col_read"])
                t_bc = sp.run(lambda e: e.dma_start(bias_col[:, :], bias), s_bc, 16)
                next_w = bias_sb[:, :].rearrange("p (i d) -> p i d", d=D)
            general_prepare(state["u_read"])
            view = load_pieces(table_in, nin, [PIECES - 1], state["u_read"], state["parts_stored"])
            t_parts, per = list(state["pieces"]), PER
            if after_loads is not None:
                after_loads()
            t_table = state["parts_stored"]
            t_x = [load_residual(x_in, 0) if x_in is not None else None]

            def aggregate(c, i):
                width = chunk_shape(c)[2]
                bank = 2 * (c % 2) + i
                pe.wait(state["agg_free"][bank])
                begin(pe, False)
                for h in range(NB):
                    k = P if h < NB - 1 else LAST
                    if h % per == 0 and c == 0 and i == 0:
                        pe.wait(t_parts[h // per])
                    if h == NB - SPILL and c == 0 and i == 0:
                        pe.wait(state["S_loaded"])
                    for part in range(NPARTS):
                        at = i * ROWW + part * D
                        first, last = h == 0 and part == 0, h == NB - 1 and part == NPARTS - 1
                        t = pe.run(lambda e, h=h, k=k, at=at, first=first, last=last: e.matmul(
                            pa[:, bank, 0:width], view[0:k, h, at:at + D], S[0:k, h, c * CW:c * CW + width],
                            start=first, stop=last), s_agg if last else None)
                end(pe)
                general_bank[0] = None
                general_chunk(c, NT + NLOOP, pa[:, bank, 0:width], s_agg, table_in, row_at=i * ROWW, ready=t_table)
                return t

            def copy_sums(c, i, t_sums):
                width, bank = chunk_shape(c)[2], 2 * (c % 2) + i
                act.wait(t_sums, state["agg_sb_read"])
                t = act.run(lambda e: e.activation(agg_sb[:, i, 0:width], pa[:, bank, 0:width], ACT.Copy), s_aggc)
                state["agg_free"][bank] = t
                return t

            def finish_fused(c, t_copied):
                nq, r, n = chunk_shape(c)
                sp.wait(state["x_read"], t_dinv_tab)
                flat = xres[:, :, :].rearrange("p q d -> p (q d)")
                row = dinv_tab[c * CW:c * CW + n].partition_broadcast(P)
                t_dr = sp.run(lambda e: e.dma_start(flat[:, 0:n], row), s_dr, 16)
                outs = []
                for o in range(2):
                    bank = state["unit"] % 2
                    state["unit"] += 1
                    pe.wait(t_w, t_copied, state["out_read"][bank])
                    for i in range(nin):
                        t = pe.run(lambda e, i=i, o=o, bank=bank: e.matmul(
                            pw[:, bank, 0:n], w_sb[:, i, o * D:(o + 1) * D], agg_sb[:, i, 0:n],
                            start=(i == 0), stop=(i == nin - 1)), s_out if i == nin - 1 else None)
                    outs.append((bank, t))
                state["w_read"] = t
                for o, (bank, _) in enumerate(outs):
                    state["out_read"][bank] = dstep(lambda e, o=o, bank=bank: e.tensor_tensor(
                        agg_sb[:, o, 0:n], pw[:, bank, 0:n], flat[:, 0:n], ALU.mult), t, t_dr)
                    act.wait(state["out_read"][bank], t_bc)
                    t_h = act.run(lambda e, o=o: e.activation(agg_sb[:, o, 0:n], agg_sb[:, o, 0:n], ACT.Relu,
                                                              bias=bias_col[:, o:o + 1]), s_a)
                state["bias_col_read"] = t_h
                state["x_read"] = wait_v()
                bank, t_out = product(c, lambda i, q, r: agg_sb[:, i, q * P:q * P + r],
                                      lambda i: next_w[:, i, :], 2, t_b, t_h)
                state["agg_sb_read"] = t_out
                state["bias_read"] = t_out
                v = views(c)[0]
                out = out_view(c, bank)
                state["out_read"][bank] = dstep(lambda e: e.tensor_tensor(v, out, dinv_of(c), ALU.mult), t_out,
                                                state["val_stored"])
                split_and_store(c, val, table_out, 0)

            def finish(c, t_copied):
                if fused:
                    finish_fused(c, t_copied)
                    return
                for half in range(nout):
                    bank, t_out = product(c, lambda i, q, r: agg_sb[:, i, q * P:q * P + r],
                                          lambda i, half=half: w_sb[:, i, half * D:(half + 1) * D],
                                          nin, t_w, t_copied)
                    state["agg_sb_read"] = state["w_read"] = t_out
                    epilogue_conv(c, half, bank, t_out, t_b, table_out, relu, t_x[0], x_out)
                if x_in is not None and c + 1 < NCH:
                    t_x[0] = load_residual(x_in, c + 1)

            pending = None
            for c in range(NCH):
                t_sums = [aggregate(c, 0)]
                final = c == NCH - 1
                if final and nin == 2:
                    t_sums.append(aggregate(c, 1))
                stored = state["parts_stored"]
                if final and next_nin:
                    load_pieces(table_out, next_nin, EARLY[:2], t_sums[-1], stored)
                if pending is not None:
                    finish(*pending)
                if final and next_nin:
                    load_pieces(table_out, next_nin, EARLY[2:], stored)
                if not final and nin == 2:
                    t_sums.append(aggregate(c, 1))
                copied = [copy_sums(c, i, t) for i, t in enumerate(t_sums)]
                state["u_read"] = t_sums[-1]
                pending = (c, copied[-1])
            finish(*pending)

        def gate():
            t_w, t_b = load_weights(a["gate_w"], 1, 1, a["gate_b"])
            t_read = [None, None]

            def load(c):
                n = chunk_shape(c)[2]
                sp.wait(t_read[c % 2])
                t_xt = sp.run(lambda e: e.dma_start(agg_sb[:, c % 2, 0:n], a["x_t"][:, c * CW:c * CW + n]),
                              s_xt[c % 2], 16)
                return t_xt, load_residual(a["x"], c)

            def one_chunk(c, t_xt, t_x):
                bank, t_out = product(c, lambda i, q, r, c=c: agg_sb[:, c % 2, q * P:q * P + r],
                                      lambda i: w_sb[:, 0, 0:D], 1, t_w, t_xt)
                t_read[c % 2] = state["agg_sb_read"] = state["w_read"] = t_out
                v, x = views(c)
                out = out_view(c, bank)
                state["out_read"][bank] = state["bias_read"] = dstep(
                    lambda e, c=c: e.tensor_tensor(v, out, bias_of(c, 0), ALU.add), t_out, t_b)
                act.wait(wait_v())
                t = act.run(lambda e, v=v: e.activation(v, v, ACT.Sigmoid), s_a)
                state["x_read"] = dstep(lambda e, v=v, x=x: e.tensor_tensor(v, v, x, ALU.mult), t, t_x)
                dstep(lambda e, v=v, c=c: e.tensor_tensor(v, v, dinv_of(c), ALU.mult), t_dinv)
                following = load(c + 1) if c + 1 < NCH else None
                split_and_store(c, val, narrow_tab[0], 0)
                return following

            loads = load(0)
            for c in range(NCH):
                before = state["parts_stored"]
                loads = one_chunk(c, *loads)
                load_early(c, before)

        def gather_groups(groups, table, t_table, coefs, accumulator, ncoef, t_acc, t_edge, between=None):
            rows_read = s_seg.value
            pool.wait(t_edge, t_table)
            dve.wait(t_edge, t_acc)
            width = ncoef * WIN

            def coefficients(g):
                b = g % 2
                if g >= 2:
                    dve.wait((s_seg.sem, rows_read + g - 1))
                off = e_off[:, GT * g:GT * (g + 1)].unsqueeze(2).to_broadcast([P, GT, WIN])
                lane = win_iota.unsqueeze(1).to_broadcast([P, GT, WIN])
                t = dve.run(lambda e: e.tensor_tensor(hot[:, b], off, lane, ALU.is_equal), s_hot)
                dve.wait(t)
                return dve.run(lambda e: coefs(e, g, b), s_hot)

            pe.wait(*state["out_read"])
            t_coef = coefficients(0)
            added = [None, None]
            for g in range(groups):
                slot = g % NRING
                if g >= NRING:
                    pool.wait((s_seg.sem, rows_read + g - NRING + 1))
                for t in range(GT):
                    index = bass.IndirectOffsetOnAxis(ap=gather_idx[:, GT * g + t:GT * g + t + 1], axis=0)
                    t_rows = pool.run(lambda e, slot=slot, t=t, index=index: e.indirect_dma_start(
                        rows[:, slot, t], None, table, index), s_rows[slot], 16)
                pe.wait(t_coef, t_rows, added[g % 2])
                for t in range(GT):
                    rhs = hot_w[:, g % 2, t] if ncoef == 1 else coef[g % 2][:, t * NJ:(t + 1) * NJ, :]
                    t_seg = pe.run(lambda e, g=g, t=t, slot=slot, rhs=rhs: e.matmul(
                        pw[:, g % 2, 0:width], rows[:, slot, t], rhs, start=(t == 0), stop=(t == GT - 1)),
                        s_seg if t == GT - 1 else None)
                if between is not None:
                    between.prepare(g)
                if g + 1 < groups:
                    t_coef = coefficients(g + 1)
                base = []

                def read_base(e, g=g, base=base):
                    base.append(e.value_load(base_i[0:1, g:g + 1], min_val=0, max_val=N - 1))

                dve.run(read_base)
                dve.wait(t_seg)
                if s_accd.value:
                    dve.wait((s_accd.sem, s_accd.value))

                def add(e, g=g, base=base):
                    first = base[0]
                    if ncoef == 1:
                        place = accumulator[:, bass.ds(first, WIN)]
                        return e.tensor_tensor(place, place, pw[:, g % 2, 0:width], ALU.add)
                    place = accumulator[:, :, bass.ds(first, WIN)]
                    sums = pw[:, g % 2, 0:width].rearrange("p (j w) -> p j w", w=WIN)
                    return e.tensor_tensor(place, place, sums, ALU.add)

                added[g % 2] = dve.run(add, s_accd)
                if between is not None:
                    between.finish(g)
            return added[(groups - 1) % 2]

        def dense_half(t_free, t_table, t_ew, t_acc):
            sp.wait(t_free, t_spill, t_tabs)
            act.wait(t_free, t_spill)
            sp.run(lambda e: e.dma_start(d_code, code_tab), s_dload, 16)
            sp.run(lambda e: e.dma_start(d_lo, lo_tab), s_dload, 16)
            sp.wait(t_table)
            full = (NB - 1) * P
            sp.run(lambda e: e.dma_start(d_x[:, 0:NB - 1, :], x_tab[0][0:full, :].rearrange("(h p) d -> p h d", p=P)),
                   s_dload, 16)
            t_load = sp.run(lambda e: e.dma_start(d_x[0:LAST, NB - 1, :], x_tab[0][full:N, :]), s_dload, 16)
            pool.wait(t_free, t_spill)
            pool.run(lambda e: e.iota(d_code_iota, pattern=[[1, CODES]], base=0, channel_multiplier=0,
                                      allow_small_or_imprecise_dtypes=True), s_lane)
            t_iota = pool.run(lambda e: e.iota(d_lo_iota, pattern=[[1, P]], base=0, channel_multiplier=0,
                                               allow_small_or_imprecise_dtypes=True), s_lane)
            w = e_w[:, NGG * GT:NT]
            cut = [d_code_hot.rearrange("p a b -> p (a b)")[:, i * DT:(i + 1) * DT] for i in range(2)]
            dve.wait(t_spill, t_ew)
            t_w = dve.chain(s_dprep, lambda e: e.tensor_copy(cut[0], w),
                            lambda e: e.tensor_copy(d_w[:, 0], cut[0]),
                            lambda e: e.tensor_tensor(d_w[:, 2], w, cut[0], ALU.subtract),
                            lambda e: e.tensor_copy(cut[1], d_w[:, 2]),
                            lambda e: e.tensor_copy(d_w[:, 1], cut[1]),
                            lambda e: e.tensor_tensor(d_w[:, 2], d_w[:, 2], cut[1], ALU.subtract))
            dve.wait(t_w, t_iota, t_load)
            act.wait(t_w)
            pe.wait(*state["agg_free"])
            win0, zero0, mm0, scale0 = s_dwin.value, s_dzero.value, s_dmm.value, s_dscale.value

            def clear(b):
                if b >= 2:
                    act.wait((s_dmm.sem, mm0 + b - 1))
                act.run(lambda e, b=b: e.activation(d_sum[b % 2].rearrange("p h d -> p (h d)"),
                                                    zero_col[:, :].to_broadcast([P, NB * BW]), ACT.Copy), s_dzero)

            def low_one_hots(k):
                b = k % NLO
                if k >= NLO:
                    act.wait((s_dwin.sem, win0 + k - NLO + 1))
                    dve.wait((s_dscale.sem, scale0 + NPARTS * GT * (k - NLO + 1)))
                lows = d_lo[:, GT * k:GT * (k + 1)].unsqueeze(2).to_broadcast([P, GT, P])
                lane = d_lo_iota.unsqueeze(1).to_broadcast([P, GT, P])
                t_low = dve.run(lambda e: e.tensor_tensor(d_lo_hot[:, b], lows, lane, ALU.is_equal), s_dhot)
                act.wait(t_low)
                for t in range(GT):
                    col, slot = GT * k + t, b * GT + t
                    for part in range(NPARTS):
                        t_scaled = act.run(lambda e, t=t, col=col, slot=slot, part=part: e.activation(
                            d_lo_w[:, slot, part], d_lo_hot[:, b, t], ACT.Copy,
                            scale=d_w[:, part, col:col + 1]), s_dscale)
                return t_scaled

            def code_one_hots(k):
                if k >= 2:
                    dve.wait((s_dwin.sem, win0 + k - 1))
                for t in range(GT):
                    col, slot = GT * k + t, (k % 2) * GT + t
                    t_code = dve.run(lambda e, col=col, slot=slot: e.tensor_scalar(
                        d_code_hot[:, slot], d_code_iota, d_code[:, col:col + 1], None, ALU.is_equal), s_dhot)
                return t_code

            lows, codes, adds = {}, {}, {}

            def windows(k):
                b, lo = k % 2, (k % NLO) * GT
                pe.wait(lows[k], codes[k], adds.get(k - 2))
                for t in range(GT):
                    for part in range(NPARTS):
                        for bank, (h0, h1) in enumerate(((0, HB), (HB, NB))):
                            last = t == GT - 1 and part == NPARTS - 1
                            pe.run(lambda e, b=b, lo=lo, t=t, part=part, bank=bank, h0=h0, h1=h1, last=last: e.matmul(
                                pa[:, 2 * b + bank, 0:(h1 - h0) * WIN], d_lo_w[:, lo + t, part],
                                d_code_hot[:, b * GT + t, h0 * WIN:h1 * WIN], start=(t == 0 and part == 0),
                                stop=last), s_dwin if last and bank == 1 else None)

            def add_window(k):
                b, batch = k % 2, k // BG
                rel = []

                def read_rel(e):
                    rel.append(e.value_load(batch_rel[0:1, k:k + 1], min_val=0, max_val=BW - WIN))

                dve.run(read_rel)
                dve.wait((s_dwin.sem, win0 + k + 1), (s_dzero.sem, zero0 + batch + 1), adds.get(k - 1))

                def step(e):
                    first = rel[0]
                    for bank, (h0, h1) in enumerate(((0, HB), (HB, NB))):
                        place = d_sum[batch % 2][:, h0:h1, bass.ds(first, WIN)]
                        sums = pa[:, 2 * b + bank, 0:(h1 - h0) * WIN].rearrange("p (h w) -> p h w", w=WIN)
                        ins = e.tensor_tensor(place, place, sums, ALU.add)
                    return ins

                adds[k] = dve.run(step, s_dadd)

            def batch_products(b):
                pe.wait(adds[(b + 1) * BG - 1], batch_added[0])
                for h in range(NB):
                    n = P if h < NB - 1 else LAST
                    pe.run(lambda e, h=h, n=n: e.matmul(pd[:, 0:BW], d_x[0:n, h, :], d_sum[b % 2][0:n, h, :],
                                                        start=(h == 0), stop=(h == NB - 1)),
                           s_dmm if h == NB - 1 else None)

            def add_batch(b):
                dve.wait((s_dmm.sem, mm0 + b + 1), (s_accd.sem, s_accd.value))

                def step(e):
                    g = NGG + b * BG
                    first = e.value_load(base_i[0:1, g:g + 1], min_val=0, max_val=N - 1)
                    place = acc[:, bass.ds(first, BW)]
                    return e.tensor_tensor(place, place, pd[:, 0:BW], ALU.add)

                batch_added[0] = dve.run(step, s_accd)

            batch_added = [None]
            pe.wait(t_load)
            clear(0)
            for k in range(NLO - 1):
                lows[k] = low_one_hots(k)
            codes[0] = code_one_hots(0)

            def prepare(i):
                if i < NDG:
                    windows(i)
                    if i % BG == 3 and i // BG + 1 < NDB:
                        clear(i // BG + 1)
                    if i + 1 < NDG:
                        codes[i + 1] = code_one_hots(i + 1)
                    if i + NLO - 1 < NDG:
                        lows[i + NLO - 1] = low_one_hots(i + NLO - 1)

            def finish(i):
                if i < NDG:
                    add_window(i)
                if i >= BG + 1 and (i - 1) % BG == 0 and (i - 1) // BG <= NDB:
                    batch_products((i - 1) // BG - 1)
                    add_batch((i - 1) // BG - 1)

            return Between(prepare, finish)


        def load_edges(t_free):
            sp.wait(t_free, t_offs)
            begin(sp, False)
            sp.run(lambda e: e.dma_start(gather_idx, a["src"][:, 0:NT].bitcast(U32)), s_eload, 16)
            t = sp.run(lambda e: e.dma_start(e_off, offset_tab), s_eload, 16)
            end(sp)
            begin(pool, False)
            pool.wait(t_free)
            t_lane = pool.run(lambda e: e.iota(win_iota, pattern=[[1, WIN]], base=0, channel_multiplier=0,
                                               allow_small_or_imprecise_dtypes=True), s_lane)
            end(pool)
            return t, t_lane

        def weighted():
            t_table = state["val_stored"]
            t_free = state["u_read"]
            t_e, t_lane = load_edges(t_free)
            t_ew = sp.run(lambda e: e.dma_start(e_w, a["w"]), s_eload2, 16)
            t_wt, t_b = load_weights(a["w_l1"], 1, 1, a["b_l1"])
            general_prepare(t_free)
            dve.wait(t_free)
            t_acc = dve.run(lambda e: e.memset(acc, 0.0), s_accz)
            dve.wait(t_ew)
            begin(dve, False)
            dve.wait(t_lane)
            end(dve)

            def coefs(e, g, b):
                w = e_w[:, GT * g:GT * (g + 1)].unsqueeze(2).to_broadcast([P, GT, WIN])
                return e.tensor_tensor(hot_w[:, b], hot[:, b], w, ALU.mult)

            for engine in (pool, dve, pe, act, sp):
                begin(engine, False)
            def fill_S(first):
                for k in range(first, min(first + 2, SPILL)):
                    h = NB - SPILL + k
                    state["S_loaded"] = act.run(lambda e, h=h, k=k: e.dma_start(S[:, h, :], S_tab[:, k, :]),
                                                s_fill, 16)

            group = dense_half(t_free, t_table, t_ew, t_acc)
            t_added = gather_groups(NGG, x_tab[0], t_table, coefs, acc, 1, t_acc, t_e, between=group)
            assert NGG >= NDG + 2
            act.wait((s_dmm.sem, s_dmm.value), (s_dadd.sem, s_dadd.value))
            fill_S(0)
            t_added = (s_accd.sem, s_accd.value)
            for engine in (pool, dve, pe, act, sp):
                end(engine)
            for engine in (pe, dve, pool):
                begin(engine, True)
            for c in range(NCH):
                width = chunk_shape(c)[2]
                t = general_chunk(c, NT, pa[:, 0, 0:width], None, x_tab[0],
                                  coef=lambda i: e_w[:, bass.ds(i, 1)], ready=t_table)
                begin(dve, True)
                dve.wait(t, t_acc)
                general_bank[0] = dve.run(lambda e, c=c, width=width: e.tensor_copy(
                    acc[:, c * CW:c * CW + width], pa[:, 0, 0:width]), s_g_vec)
                end(dve)
            for engine in (pe, dve, pool):
                end(engine)
            begin(pe, False)
            pe.wait(t_added)
            end(pe)
            begin(pe, True)
            pe.wait(general_bank[0])
            end(pe)
            t_ahead = [load_ahead(x_tab[0], 0), load_ahead(x_tab[0], 1)]

            def one_chunk(c):
                bank, t_out = product(c, lambda i, q, r, c=c: acc[:, c * CW + q * P:c * CW + q * P + r],
                                      lambda i: w_sb[:, 0, 0:D], 1, t_wt, t_acc)
                state["w_read"] = state["u_read"] = t_out
                v, x = views(c)
                out = out_view(c, bank)
                state["out_read"][bank] = state["bias_read"] = dstep(
                    lambda e, v=v, out=out, c=c: e.tensor_tensor(v, out, bias_of(c, 0), ALU.add), t_out, t_b,
                    state["val_stored"])
                state["ahead_read"][c % 2] = dstep(
                    lambda e, v=v, c=c: e.tensor_tensor(v, v, ahead_view(c), ALU.add), t_ahead[c])
                if c + 2 < NCH:
                    t_ahead.append(load_ahead(x_tab[0], c + 2))
                layer_norm(c)
                store_val(c, x_tab[1])
                dstep(lambda e, v=v, x=x, c=c: e.tensor_tensor(x, v, dinv_of(c), ALU.mult), state["x_read"])
                split_and_store(c, xres, narrow_tab[0], 0)
                state["x_read"] = wait_v()

            state["u_read"] = None
            for c in range(NCH):
                before = state["parts_stored"]
                one_chunk(c)
                load_early(c, before)
                if c * 2 + 2 < SPILL:
                    begin(act, False)
                    fill_S(2 * c + 2)
                    end(act)

        def tensor_product():
            t_table = state["val_stored"]
            t_free = state["u_read"]
            t_e, t_lane = load_edges(t_free)
            general_prepare(t_free)
            sp.wait(t_free)
            sp.run(lambda e: e.dma_start(attr, a["attr"]), s_eload2, 16)
            sp.run(lambda e: e.dma_start(path_w, a["path_w"]), s_eload2, 16)
            t_attr = sp.run(lambda e: e.dma_start(path_c, a["path_c"]), s_eload2, 16)
            dve.wait(t_free)
            act.wait(t_free)
            for j in range(NJ):
                if j < 5:
                    t_acc = dve.run(lambda e, j=j: e.memset(acc_j[:, j], 0.0), s_accz)
                else:
                    t_acc_act = act.run(lambda e, j=j: e.activation(
                        acc_j[:, j], zero_col[:, :].to_broadcast([P, SW]), ACT.Copy), s_accza)
            dve.wait(t_acc_act, t_attr)
            begin(dve, False)
            dve.wait(t_lane)
            end(dve)

            def coefs(e, g, b):
                h = hot[:, b].unsqueeze(2).to_broadcast([P, GT, NJ, WIN])
                at = attr[:, GT * g:GT * (g + 1), :].unsqueeze(3).to_broadcast([P, GT, NJ, WIN])
                return e.tensor_tensor(coef[b].rearrange("p (t j) w -> p t j w", t=GT), h, at, ALU.mult)

            def matrices():
                for j in range(NJ):
                    dve.run(lambda e, j=j: e.tensor_scalar(K_mat[:, j, 0:32], path_w[:, 0], path_c[:, j, 0:1], None,
                                                           ALU.mult), s_kmat)
                    for k in range(3):
                        src = path_w[:, 1 if j < 4 else 2]
                        t_k = dve.run(lambda e, j=j, k=k, src=src: e.tensor_scalar(
                            K_mat[:, j, 32 + k:D:3], src, path_c[:, j, 1 + k:2 + k], None, ALU.mult), s_kmat)

                return t_k

            def one_chunk(c, t_k):
                bank, t_out = product(c, lambda j, q, r: acc_j[:, j, c * CW + q * P:c * CW + q * P + r],
                                      lambda j: K_mat[:, j, :], NJ, t_k, None, psum=pa)
                v, x = views(c)
                out = out_view(c, bank, pa)
                t = dstep(lambda e: e.scalar_tensor_tensor(
                    out=v, in0=out, scalar=NEIGHBORS ** -0.5, in1=ahead_view(c), op0=ALU.mult, op1=ALU.add),
                    t_out, t_ahead[c], state["val_stored"])
                state["out_read"][bank] = state["ahead_read"][c % 2] = t
                if c + 2 < NCH:
                    t_ahead.append(load_ahead(x_tab[2], c + 2))
                layer_norm(c)
                store_val(c, a["out"])

            sp.wait(t_table)
            t_ahead = [load_ahead(x_tab[2], 0), load_ahead(x_tab[2], 1)]
            everyone = (pool, dve, pe, act, sp)
            before = [(x, x.value) for x in counters]
            state_before = {k: list(x) if isinstance(x, list) else x for k, x in state.items()}
            for engine in everyone:
                begin(engine, False)
            done = []

            def after_group(g):
                if g == 0:
                    done.append(matrices())
                    pe.wait(*state["agg_free"])
                for c in range(NCH):
                    if CHUNK_DONE[c] == g:
                        pe.wait((s_accd.sem, s_accd.value))
                        one_chunk(c, done[0])

            gather_groups(NG, x_tab[2], t_table, coefs, acc_j, NJ, t_acc, t_e, between=Between(lambda g: None, after_group))
            sp.wait(state["val_stored"])
            for engine in everyone:
                end(engine)
            for x, value in before:
                x.value = value
            state.update(state_before)
            del t_ahead[2:]
            for engine in everyone:
                begin(engine, True)
            t_k = matrices()
            attr_flat = attr.rearrange("p t j -> p (t j)")
            for j in range(NJ):
                for c in range(NCH):
                    width = chunk_shape(c)[2]
                    t = general_chunk(c, NT, pa[:, 0, 0:width], None, x_tab[2],
                                      coef=lambda i, j=j: attr_flat[:, bass.ds(i * NJ + j, 1)], ready=t_table)
                    dve.wait(t, t_acc)
                    general_bank[0] = dve.run(lambda e, c=c, j=j, width=width: e.tensor_copy(
                        acc_j[:, j, c * CW:c * CW + width], pa[:, 0, 0:width]), s_g_vec)
            pe.wait(general_bank[0])
            for c in range(NCH):
                one_chunk(c, t_k)
            sp.wait(state["val_stored"])
            for engine in everyone:
                end(engine)

        gate()
        def spill():
            begin(sp, False)
            sp.wait(t_S)
            for h in range(NB - SPILL, NB):
                k = h - (NB - SPILL)
                spilled.append(sp.run(lambda e, h=h, k=k: e.dma_start(S_tab[:, k, :], S[:, h, :]), s_spill, 16))
            end(sp)

        spilled = []
        convolution(narrow_tab[0], 1, 1, a["w_l0_1"], a["b_l0_1"], table_out=narrow_tab[1], next_nin=1,
                    after_loads=spill)
        t_spill = spilled[-1]
        convolution(narrow_tab[1], 1, 1, a["w_l0_2"], a["b_l0_2"], x_in=a["x"], x_out=x_tab[0])
        weighted()
        convolution(narrow_tab[0], 1, 2, a["w_l2_0"], a["b_l2_0"], table_out=wide_tab[0], next_nin=2)
        convolution(wide_tab[0], 2, 2, a["w_l2_1"], a["b_l2_1"], table_out=wide_tab[1],
                    next_nin=2)
        convolution(wide_tab[1], 2, 2, a["w_l2_2"], a["b_l2_2"], table_out=narrow_tab[0],
                    next_weights=a["w_l2_3"], next_nin=1)
        convolution(narrow_tab[0], 1, 1, a["eye"], a["b_l2_3"], relu=True, x_in=x_tab[1], x_out=x_tab[2])
        tensor_product()

        block = ctx.enter_context(nc.Block())
        block.sync(sp.emit)
        block.scalar(act.emit)
        block.vector(dve.emit)
        block.gpsimd(pool.emit)
        block.tensor(pe.emit)


def coupling_constants():
    from math import factorial

    import numpy as np

    def cg(j1, m1, j2, m2, j3, m3):
        if m3 != m1 + m2:
            return 0.0
        f = lambda n: factorial(round(n))
        c = ((2.0 * j3 + 1.0) * f(j3 + j1 - j2) * f(j3 - j1 + j2) * f(j1 + j2 - j3) * f(j3 + m3) * f(j3 - m3)
             / (f(j1 + j2 + j3 + 1) * f(j1 - m1) * f(j1 + m1) * f(j2 - m2) * f(j2 + m2))) ** 0.5
        s = 0
        for v in range(max(-j1 + j2 + m3, -j1 + m1, 0), min(j2 + j3 + m1, j3 - j1 + j2, j3 + m3) + 1):
            s += ((-1) ** (v + j2 + m2) * f(j2 + j3 + m1 - v) * f(j1 - m1 + v)
                  / (f(v) * f(j3 - j1 + j2 - v) * f(j3 + m3 - v) * f(v + j1 - j2 - m3)))
        return float(c * s)

    def real_to_complex(l):
        q = np.zeros((2 * l + 1, 2 * l + 1), dtype=np.complex128)
        for m in range(-l, 0):
            q[l + m, l + abs(m)] = 1 / np.sqrt(2)
            q[l + m, l - abs(m)] = -1j / np.sqrt(2)
        q[l, l] = 1
        for m in range(1, l + 1):
            q[l + m, l + abs(m)] = (-1) ** m / np.sqrt(2)
            q[l + m, l - abs(m)] = 1j * (-1) ** m / np.sqrt(2)
        return (-1j) ** l * q

    def wigner(l1, l2, l3):
        c = np.zeros((2 * l1 + 1, 2 * l2 + 1, 2 * l3 + 1))
        for m1 in range(-l1, l1 + 1):
            for m2 in range(-l2, l2 + 1):
                if abs(m1 + m2) <= l3:
                    c[l1 + m1, l2 + m2, l3 + m1 + m2] = cg(l1, m1, l2, m2, l3, m1 + m2)
        r = np.real(np.einsum("ij,kl,mn,ikn->jlm", real_to_complex(l1), real_to_complex(l2),
                              np.conj(real_to_complex(l3).T), c.astype(np.complex128)))
        return r / np.linalg.norm(r)

    mul = D // 4
    to_scalar, to_vector = (1 / (2 * mul)) ** 0.5, (3 / (3 * mul)) ** 0.5
    out = np.zeros((D, NJ, 4))
    comp = np.arange(3 * mul) % 3
    out[:mul, 0, 0] = wigner(0, 0, 0)[0, 0, 0] * to_scalar
    for k in range(3):
        for j in range(3):
            out[:mul, 1 + j, 1 + k] = wigner(0, 1, 1)[0, j, k] * to_vector
        out[mul:, 0, 1 + k] = wigner(1, 0, 1)[comp, 0, k] * to_vector
        out[mul:, 1 + k, 0] = wigner(1, 1, 0)[comp, k, 0] * to_scalar
        for j in range(5):
            out[mul:, 4 + j, 1 + k] = wigner(1, 2, 1)[comp, j, k] * to_vector
    return out.astype(np.float32)


def kernel(**inputs):
    import numpy as np
    import concourse.bacc as bacc
    from concourse.bass_utils import run_bass_kernel_spmd

    v = {k: np.asarray(x) for k, x in inputs.items()}
    src = np.zeros(NT * P, v["src"].dtype)
    dst = np.full(NT * P, FAR, v["dst"].dtype)
    src[:E], dst[:E] = v["src"], v["dst"]
    loop_src = np.zeros(NLOOP * P, v["src"].dtype)
    loop_dst = np.full(NLOOP * P, FAR, v["dst"].dtype)
    loop_src[:N] = loop_dst[:N] = np.arange(N)
    tiles = lambda x: np.ascontiguousarray(x.reshape(-1, P).T)
    w = np.zeros(NT * P, v["edge_weight"].dtype)
    w[:E] = v["edge_weight"]
    attr = np.zeros((NT * P, NJ), v["edge_attr_9"].dtype)
    attr[:E] = v["edge_attr_9"]
    row = lambda b: np.ascontiguousarray(np.broadcast_to(b, (P, b.shape[-1])))
    wide = lambda m: np.ascontiguousarray(m.reshape(-1, P, m.shape[-1]).transpose(1, 0, 2))
    mats = [v[f"L3_gnn_w{i}"][:, 0, :] for i in range(5)]
    stack = lambda s, m: np.concatenate([mats[s], np.repeat(mats[m], 3, axis=0)], axis=0)
    arrays = {
        "x": v["x"], "x_t": np.ascontiguousarray(v["x"].T),
        "src": tiles(np.concatenate([src, loop_src])), "dst": tiles(np.concatenate([dst, loop_dst])),
        "w": tiles(w), "attr": np.ascontiguousarray(attr.reshape(NT, P, NJ).transpose(1, 0, 2)),
        "gate_w": wide(v["L0_gnn_gate_W"]), "gate_b": row(v["L0_gnn_gate_b"]),
        "w_l0_1": wide(v["L0_gnn_W1"]), "b_l0_1": row(v["L0_gnn_b1"]),
        "w_l0_2": wide(v["L0_gnn_W2"]), "b_l0_2": row(v["L0_gnn_b2"]),
        "w_l1": wide(v["L1_gnn_W"].T), "b_l1": row(v["L1_gnn_b"]),
        **{f"w_l2_{i}": wide(v[f"L2_gnn_W{i}"]) for i in range(4)},
        **{f"b_l2_{i}": row(v[f"L2_gnn_b{i}"]) for i in range(4)},
        "b_l2_2": np.ascontiguousarray(v["L2_gnn_b2"].reshape(2, P).T), "eye": wide(np.eye(P, dtype=np.float32)),
        "path_w": np.ascontiguousarray(np.stack([stack(0, 3), stack(1, 2), stack(1, 4)], axis=1)),
        "path_c": coupling_constants(),
    }
    nc = bacc.Bacc("TRN2", target_bir_lowering=False, num_devices=1)
    args = {k: nc.dram_tensor(f"in_{k}", x.shape, mybir.dt.from_np(x.dtype), kind="ExternalInput").ap()
            for k, x in arrays.items()}
    args["out"] = nc.dram_tensor("out", (N, D), F32, kind="ExternalOutput").ap()
    build_program(nc, args)
    r = run_bass_kernel_spmd(nc, [{f"in_{k}": x for k, x in arrays.items()}], core_ids=[0])
    return r.results[0]["out"]
```
